# Optimizing a Trainium2 kernel written in Bass

```python
import numpy as np
import jax
import jax.numpy as jnp

def _softmax(x, axis=-1):
    return jax.nn.softmax(x, axis=axis)
def _gelu(x):
    return jax.nn.gelu(x, approximate=True)
def _silu(x):
    return jax.nn.silu(x)
def _sigmoid(x):
    return jax.nn.sigmoid(x)
def _layernorm(x, axis=-1, eps=1e-5):
    m = jnp.mean(x, axis=axis, keepdims=True)
    v = jnp.var(x, axis=axis, keepdims=True)
    return (x - m) / jnp.sqrt(v + eps)
def _scatter_add(tgt, idx, src, axis=0):
    return tgt.at[idx].add(src)
def _segment_sum(src, seg, n):
    return jax.ops.segment_sum(src, seg, n)

kernel_name = 'mk_conv_seq_d2_conv_nhwc64_3f072b'

def setup_inputs(seed: int = 0):
    np.random.seed(seed)
    _w = jnp.asarray
    def _rec_inputs():
        import jax
        import jax.numpy as jnp
        _gk = jax.random.key(seed)
        x = -0.0005207 + 1.001 * jax.random.normal(jax.random.fold_in(_gk, 1), (2, 256, 64, 64), jnp.float32)
        return x
    x = _rec_inputs()
    def _L0_conv_setup():
        import jax, jax.numpy as jnp
        import numpy as np
        B, C, H, W = (2, 256, 64, 64)
        CH = C // 2

        def conv1x1(x, w, b):
            return jnp.einsum('oc,bchw->bohw', w, x) + b[None, :, None, None]
        key = jax.random.key(seed)
        ks = jax.random.split(key, 9)
        s_in = 1.0 / np.sqrt(C)
        s_h = 1.0 / np.sqrt(CH)
        return {'inp': jax.random.normal(ks[0], (B, C, H, W), jnp.float32), 'w_theta': jax.random.normal(ks[1], (CH, C), jnp.float32) * s_in, 'b_theta': jax.random.normal(ks[2], (CH,), jnp.float32) * 0.01, 'w_phi': jax.random.normal(ks[3], (CH, C), jnp.float32) * s_in, 'b_phi': jax.random.normal(ks[4], (CH,), jnp.float32) * 0.01, 'w_g': jax.random.normal(ks[5], (CH, C), jnp.float32) * s_in, 'b_g': jax.random.normal(ks[6], (CH,), jnp.float32) * 0.01, 'w_out': jax.random.normal(ks[7], (C, CH), jnp.float32) * s_h, 'b_out': jax.random.normal(ks[8], (C,), jnp.float32) * 0.01}
    _L0_conv_all = _L0_conv_setup()
    _L0_conv_in = {k: v for k, v in _L0_conv_all.items() if k in ('w_theta', 'b_theta', 'w_phi', 'b_phi', 'w_g', 'b_g', 'w_out', 'b_out', )}
    del _L0_conv_all

    def _L1_conv_setup():
        import jax, jax.numpy as jnp
        import numpy as np
        WS = 8
        NH = 8
        SCALE = 4.0
        GK = 9
        EPS = 1e-05

        def _rel_pos_index(ws):
            coords = np.stack(np.meshgrid(np.arange(ws), np.arange(ws), indexing='ij'))
            cf = coords.reshape(2, -1)
            rel = (cf[:, :, None] - cf[:, None, :]).transpose(1, 2, 0).astype(np.int64)
            rel[..., 0] += ws - 1
            rel[..., 1] += ws - 1
            rel[..., 0] *= 2 * ws - 1
            return jnp.asarray(rel.sum(-1))

        def _ln(x, g, b):
            m = x.mean(-1, keepdims=True)
            v = ((x - m) ** 2).mean(-1, keepdims=True)
            return (x - m) / jnp.sqrt(v + EPS) * g + b

        def _forward(x, norm1_g, norm1_b, qkv_w, qkv_b, rpb_table, proj_w, proj_b, gaze_w, gaze_b, norm2_g, norm2_b, fc1_w, fc1_b, fc2_w, fc2_b, H, W):
            B, C, _, _ = x.shape
            hd = C // NH
            nw = H // WS
            N = WS * WS
            xf = x.transpose(0, 2, 3, 1).reshape(B, H * W, C)
            shortcut = xf
            xn = _ln(xf, norm1_g, norm1_b).reshape(B, H, W, C)
            xw = xn.reshape(B, nw, WS, nw, WS, C).transpose(0, 1, 3, 2, 4, 5).reshape(B * nw * nw, N, C)
            qkv = (xw @ qkv_w.T + qkv_b).reshape(-1, N, 3, NH, hd).transpose(2, 0, 3, 1, 4)
            q, k, v = (qkv[0] * SCALE, qkv[1], qkv[2])
            attn = jnp.einsum('whnd,whmd->whnm', q, k)
            rpi = _rel_pos_index(WS)
            bias = rpb_table[rpi.reshape(-1)].reshape(N, N, NH).transpose(2, 0, 1)
            attn = jax.nn.softmax(attn + bias[None], axis=-1)
            out = jnp.einsum('whnm,whmd->whnd', attn, v).transpose(0, 2, 1, 3).reshape(-1, N, C)
            v6 = v.reshape(B, nw, nw, NH, WS, WS, hd)
            img = v6.transpose(0, 4, 1, 5, 2, 3, 6).reshape(B, H, W, C)
            pad = GK // 2
            img = jax.lax.conv_general_dilated(img, gaze_w, (1, 1), ((pad, pad), (pad, pad)), dimension_numbers=('NHWC', 'HWIO', 'NHWC'), feature_group_count=C) + gaze_b
            gz = img.reshape(B, WS, nw, WS, nw, C).transpose(0, 2, 4, 1, 3, 5).reshape(B * nw * nw, N, C)
            out = (out + gz) @ proj_w.T + proj_b
            xr = out.reshape(B, nw, nw, WS, WS, C).transpose(0, 1, 3, 2, 4, 5).reshape(B, H * W, C)
            xf = shortcut + xr
            h = _ln(xf, norm2_g, norm2_b)
            h = jax.nn.gelu(h @ fc1_w.T + fc1_b, approximate=False) @ fc2_w.T + fc2_b
            xf = xf + h
            return xf.reshape(B, H, W, C).transpose(0, 3, 1, 2)
        key = jax.random.key(seed)
        ks = jax.random.split(key, 8)
        C, H, W, B, HID = (256, 64, 64, 16, 1024)
        return {'H': 64, 'W': 64, 'x': jax.random.normal(ks[0], (B, C, H, W), jnp.float32), 'norm1_g': jnp.ones((C,), jnp.float32), 'norm1_b': jnp.zeros((C,), jnp.float32), 'qkv_w': jax.random.normal(ks[1], (3 * C, C), jnp.float32) * 0.02, 'qkv_b': jnp.zeros((3 * C,), jnp.float32), 'rpb_table': jax.random.normal(ks[2], (225, NH), jnp.float32) * 0.02, 'proj_w': jax.random.normal(ks[3], (C, C), jnp.float32) * 0.02, 'proj_b': jnp.zeros((C,), jnp.float32), 'gaze_w': jax.random.normal(ks[4], (GK, GK, 1, C), jnp.float32) * 0.02, 'gaze_b': jnp.zeros((C,), jnp.float32), 'norm2_g': jnp.ones((C,), jnp.float32), 'norm2_b': jnp.zeros((C,), jnp.float32), 'fc1_w': jax.random.normal(ks[5], (HID, C), jnp.float32) * 0.02, 'fc1_b': jnp.zeros((HID,), jnp.float32), 'fc2_w': jax.random.normal(ks[6], (C, HID), jnp.float32) * 0.02, 'fc2_b': jnp.zeros((C,), jnp.float32)}
    _L1_conv_all = _L1_conv_setup()
    _L1_conv_in = {k: v for k, v in _L1_conv_all.items() if k in ('norm1_g', 'norm1_b', 'qkv_w', 'qkv_b', 'rpb_table', 'proj_w', 'proj_b', 'gaze_w', 'gaze_b', 'norm2_g', 'norm2_b', 'fc1_w', 'fc1_b', 'fc2_w', 'fc2_b', )}
    del _L1_conv_all

    return {
        "x": x,
        "L0_conv_w_theta": _L0_conv_in["w_theta"],
        "L0_conv_b_theta": _L0_conv_in["b_theta"],
        "L0_conv_w_phi": _L0_conv_in["w_phi"],
        "L0_conv_b_phi": _L0_conv_in["b_phi"],
        "L0_conv_w_g": _L0_conv_in["w_g"],
        "L0_conv_b_g": _L0_conv_in["b_g"],
        "L0_conv_w_out": _L0_conv_in["w_out"],
        "L0_conv_b_out": _L0_conv_in["b_out"],
        "L1_conv_norm1_g": _L1_conv_in["norm1_g"],
        "L1_conv_norm1_b": _L1_conv_in["norm1_b"],
        "L1_conv_qkv_w": _L1_conv_in["qkv_w"],
        "L1_conv_qkv_b": _L1_conv_in["qkv_b"],
        "L1_conv_rpb_table": _L1_conv_in["rpb_table"],
        "L1_conv_proj_w": _L1_conv_in["proj_w"],
        "L1_conv_proj_b": _L1_conv_in["proj_b"],
        "L1_conv_gaze_w": _L1_conv_in["gaze_w"],
        "L1_conv_gaze_b": _L1_conv_in["gaze_b"],
        "L1_conv_norm2_g": _L1_conv_in["norm2_g"],
        "L1_conv_norm2_b": _L1_conv_in["norm2_b"],
        "L1_conv_fc1_w": _L1_conv_in["fc1_w"],
        "L1_conv_fc1_b": _L1_conv_in["fc1_b"],
        "L1_conv_fc2_w": _L1_conv_in["fc2_w"],
        "L1_conv_fc2_b": _L1_conv_in["fc2_b"],
    }

def reference(x, L0_conv_w_theta, L0_conv_b_theta, L0_conv_w_phi, L0_conv_b_phi, L0_conv_w_g, L0_conv_b_g, L0_conv_w_out, L0_conv_b_out, L1_conv_norm1_g, L1_conv_norm1_b, L1_conv_qkv_w, L1_conv_qkv_b, L1_conv_rpb_table, L1_conv_proj_w, L1_conv_proj_b, L1_conv_gaze_w, L1_conv_gaze_b, L1_conv_norm2_g, L1_conv_norm2_b, L1_conv_fc1_w, L1_conv_fc1_b, L1_conv_fc2_w, L1_conv_fc2_b):
    import jax
    import jax.numpy as jnp
    def _L0_conv_ref(inp, w_theta, b_theta, w_phi, b_phi, w_g, b_g, w_out, b_out):
        import jax, jax.numpy as jnp
        import numpy as np
        B, C, H, W = (2, 256, 64, 64)
        CH = C // 2

        def conv1x1(x, w, b):
            return jnp.einsum('oc,bchw->bohw', w, x) + b[None, :, None, None]
        theta = conv1x1(inp, w_theta, b_theta)
        phi = conv1x1(inp, w_phi, b_phi)
        g = conv1x1(inp, w_g, b_g)
        L = CH * H
        th = theta.reshape(B, L, W)
        ph = jnp.swapaxes(phi.reshape(B, L, W), 1, 2)
        gg = g.reshape(B, L, W)
        attn = jax.nn.softmax(jnp.matmul(th, ph), axis=-1)
        o = jnp.matmul(attn, gg).reshape(B, CH, H, W)
        return conv1x1(o, w_out, b_out) + inp

    def _L1_conv_ref(H, W, x, norm1_g, norm1_b, qkv_w, qkv_b, rpb_table, proj_w, proj_b, gaze_w, gaze_b, norm2_g, norm2_b, fc1_w, fc1_b, fc2_w, fc2_b):
        import jax, jax.numpy as jnp
        import numpy as np
        WS = 8
        NH = 8
        SCALE = 4.0
        GK = 9
        EPS = 1e-05

        def _rel_pos_index(ws):
            coords = np.stack(np.meshgrid(np.arange(ws), np.arange(ws), indexing='ij'))
            cf = coords.reshape(2, -1)
            rel = (cf[:, :, None] - cf[:, None, :]).transpose(1, 2, 0).astype(np.int64)
            rel[..., 0] += ws - 1
            rel[..., 1] += ws - 1
            rel[..., 0] *= 2 * ws - 1
            return jnp.asarray(rel.sum(-1))

        def _ln(x, g, b):
            m = x.mean(-1, keepdims=True)
            v = ((x - m) ** 2).mean(-1, keepdims=True)
            return (x - m) / jnp.sqrt(v + EPS) * g + b

        def _forward(x, norm1_g, norm1_b, qkv_w, qkv_b, rpb_table, proj_w, proj_b, gaze_w, gaze_b, norm2_g, norm2_b, fc1_w, fc1_b, fc2_w, fc2_b, H, W):
            B, C, _, _ = x.shape
            hd = C // NH
            nw = H // WS
            N = WS * WS
            xf = x.transpose(0, 2, 3, 1).reshape(B, H * W, C)
            shortcut = xf
            xn = _ln(xf, norm1_g, norm1_b).reshape(B, H, W, C)
            xw = xn.reshape(B, nw, WS, nw, WS, C).transpose(0, 1, 3, 2, 4, 5).reshape(B * nw * nw, N, C)
            qkv = (xw @ qkv_w.T + qkv_b).reshape(-1, N, 3, NH, hd).transpose(2, 0, 3, 1, 4)
            q, k, v = (qkv[0] * SCALE, qkv[1], qkv[2])
            attn = jnp.einsum('whnd,whmd->whnm', q, k)
            rpi = _rel_pos_index(WS)
            bias = rpb_table[rpi.reshape(-1)].reshape(N, N, NH).transpose(2, 0, 1)
            attn = jax.nn.softmax(attn + bias[None], axis=-1)
            out = jnp.einsum('whnm,whmd->whnd', attn, v).transpose(0, 2, 1, 3).reshape(-1, N, C)
            v6 = v.reshape(B, nw, nw, NH, WS, WS, hd)
            img = v6.transpose(0, 4, 1, 5, 2, 3, 6).reshape(B, H, W, C)
            pad = GK // 2
            img = jax.lax.conv_general_dilated(img, gaze_w, (1, 1), ((pad, pad), (pad, pad)), dimension_numbers=('NHWC', 'HWIO', 'NHWC'), feature_group_count=C) + gaze_b
            gz = img.reshape(B, WS, nw, WS, nw, C).transpose(0, 2, 4, 1, 3, 5).reshape(B * nw * nw, N, C)
            out = (out + gz) @ proj_w.T + proj_b
            xr = out.reshape(B, nw, nw, WS, WS, C).transpose(0, 1, 3, 2, 4, 5).reshape(B, H * W, C)
            xf = shortcut + xr
            h = _ln(xf, norm2_g, norm2_b)
            h = jax.nn.gelu(h @ fc1_w.T + fc1_b, approximate=False) @ fc2_w.T + fc2_b
            xf = xf + h
            return xf.reshape(B, H, W, C).transpose(0, 3, 1, 2)
        return _forward(x, norm1_g, norm1_b, qkv_w, qkv_b, rpb_table, proj_w, proj_b, gaze_w, gaze_b, norm2_g, norm2_b, fc1_w, fc1_b, fc2_w, fc2_b, H, W)

    def _gn(v, G=32, eps=1e-5):
        B_, H_, W_, C_ = v.shape
        g = v.reshape(B_, H_, W_, G, C_ // G)
        m = jnp.mean(g, axis=(1, 2, 4), keepdims=True)
        s = jnp.var(g, axis=(1, 2, 4), keepdims=True)
        return ((g - m) / jnp.sqrt(s + eps)).reshape(v.shape)

    def _ln_c(v, eps=1e-6):
        m = jnp.mean(v, axis=-1, keepdims=True)
        s = jnp.var(v, axis=-1, keepdims=True)
        return (v - m) / jnp.sqrt(s + eps)

    def _ln_t(v, eps=1e-5):
        m = jnp.mean(v, axis=-1, keepdims=True)
        s = jnp.var(v, axis=-1, keepdims=True)
        return (v - m) / jnp.sqrt(s + eps)

    def _to_tokens(v):
        B_, H_, W_, C_ = v.shape
        return v.reshape(B_, H_ * W_, C_)
    def _from_tokens(t, like):
        return t.reshape(like.shape)

    x = _L0_conv_ref(x, L0_conv_w_theta, L0_conv_b_theta, L0_conv_w_phi, L0_conv_b_phi, L0_conv_w_g, L0_conv_b_g, L0_conv_w_out, L0_conv_b_out)
    x = _L1_conv_ref(64, 64, x, L1_conv_norm1_g, L1_conv_norm1_b, L1_conv_qkv_w, L1_conv_qkv_b, L1_conv_rpb_table, L1_conv_proj_w, L1_conv_proj_b, L1_conv_gaze_w, L1_conv_gaze_b, L1_conv_norm2_g, L1_conv_norm2_b, L1_conv_fc1_w, L1_conv_fc1_b, L1_conv_fc2_w, L1_conv_fc2_b)
    return x


_drawn_inputs = setup_inputs


def setup_inputs(seed=0):
    import zlib

    import numpy as np

    out = dict(_drawn_inputs(seed))
    spreads = {'L1_conv_norm1_g': (1.0, 0.6),
     'L1_conv_norm1_b': (0.0, 0.8),
     'L1_conv_qkv_b': (0.0, 0.1),
     'L1_conv_proj_b': (0.0, 0.1),
     'L1_conv_gaze_b': (0.0, 0.288),
     'L1_conv_norm2_g': (1.0, 0.6),
     'L1_conv_norm2_b': (0.0, 0.8),
     'L1_conv_fc1_b': (0.0, 0.276),
     'L1_conv_fc2_b': (0.0, 0.1)}
    factors = {'L0_conv_b_theta': 2.995,
     'L0_conv_b_phi': 2.904,
     'L0_conv_b_g': 8.0,
     'L0_conv_b_out': 7.353,
     'L1_conv_rpb_table': 64.0,
     'L1_conv_gaze_w': 3.598}
    for name, (base, spread) in spreads.items():
        noise = np.random.default_rng([zlib.crc32(name.encode()), seed]).standard_normal(out[name].shape)
        drawn = base * np.exp(spread * noise) if base else spread * noise
        out[name] = jnp.asarray(drawn.astype(out[name].dtype))
    for name, factor in factors.items():
        out[name] = (out[name] * factor).astype(out[name].dtype)
    return out
```

```python
from contextlib import ExitStack

import concourse.bass as bass
from concourse import mybir

F32 = mybir.dt.float32
BF16 = mybir.dt.bfloat16
ALU = mybir.AluOpType
ACT = mybir.ActivationFunctionType
X = mybir.AxisListType.X

P = 128
B, C, H, W = 2, 256, 64, 64
PIX = H * W
CH = C // 2
KT = C // P
LK = CH * H
HALF = W
CHUNK = 512
ROWS = CHUNK // W
CHUNKS = PIX // CHUNK
GROUP = 512
QT = GROUP // P
GROUPS = LK // GROUP
UNITS = LK // (2 * P)
MAXCH = QT * LK // 512
KCH = LK // 512
LOOKED = 8
TURNS = 7

WS = 8
NH = 8
HD = C // NH
HP = NH // 2
HID = 1024
FT = HID // P
GK = 9
PADW = W + GK - 1
EPS = 1e-5
SCALE = 4.0

VEC = {}
_n = 0
for _name, _w in (("b_g", 1), ("b_out", KT), ("norm1_g", KT), ("norm1_b", KT), ("qkv_b", 3 * KT), ("proj_b", KT),
                  ("gaze_b", KT), ("norm2_g", KT), ("norm2_b", KT), ("fc1_b", FT), ("fc2_b", KT)):
    VEC[_name] = _n
    _n += _w
NVEC = _n


def nonlocal_part(nc, x, wqk, bqk, wg, wout, vec, ident, x1):
    with ExitStack() as ctx:
        def sb(name, shape, dt=F32):
            return ctx.enter_context(nc.sbuf_tensor(name, shape, dt))

        def sem(name):
            return ctx.enter_context(nc.semaphore(name))

        wqk_sb = sb("wqk_sb", [P, KT, 2 * CH])
        bqk_sb = sb("bqk_sb", [P, 2 * CH])
        wg_sb = sb("wg_sb", [P, KT, CH])
        wout_sb = sb("wout_sb", [P, C])
        vec_sb = sb("vec_sb1", [P, NVEC])
        ident_sb = sb("ident_sb1", [P, P])
        x_ring = sb("x_ring", [P, 2, KT, ROWS, 2, W])
        proj = sb("proj", [P, 2, 2, 2 * CH])
        q1 = sb("q1", [P, LK], BF16)
        q2 = sb("q2", [P, LK], BF16)
        kh = sb("kh", [P, LK], BF16)
        kl = sb("kl", [P, LK], BF16)
        g_sb = sb("g_sb", [P, H, W + 1])
        probs = sb("probs", [P, 2, 2 * GROUP])
        chunk_max = sb("chunk_max", [P, KCH, QT])
        qmax = sb("qmax", [P, QT])
        neg_max = sb("neg_max", [P, QT])
        rden = sb("rden", [P, QT])
        o_grp = sb("o_grp", [P, QT * W])
        x_res = sb("x_res", [P, KT, QT * W])
        y = sb("y", [P, KT, QT * W])

        sT = ctx.enter_context(nc.psum_tensor("sT", [P, 2, 2, 512], F32))
        s_max = ctx.enter_context(nc.psum_tensor("s_max", [P, 2, 512], F32))
        acc = ctx.enter_context(nc.psum_tensor("acc", [P, 512], F32))
        misc = ctx.enter_context(nc.psum_tensor("misc", [P, 512], F32))

        weights_landed = sem("weights_landed")
        x_landed = [sem("x_landed0"), sem("x_landed1")]
        qk_projected = sem("qk_projected")
        qk_biased = sem("qk_biased")
        high_done = sem("high_done")
        split_done = sem("split_done")
        g_projected = sem("g_projected")
        g_ready = sem("g_ready")
        kl_zeroed = sem("kl_zeroed")
        max_scored = sem("max_scored")
        max_free = sem("max_free")
        qmax_done = sem("qmax_done")
        neg_ready = sem("neg_ready")
        row_done = sem("row_done")
        row_high = sem("row_high")
        shift_ready = sem("shift_ready")
        scored = sem("scored")
        probs_ready = sem("probs_ready")
        pv_done = sem("pv_done")
        rden_done = sem("rden_done")
        normed = sem("normed")
        out_projected = sem("out_projected")
        res_landed = sem("res_landed")
        y_ready = sem("y_ready")
        y_stored = sem("y_stored")

        LOADS = 6
        block = ctx.enter_context(nc.Block())

        @block.sync
        def _(sp):
            for dst, src in ((wqk_sb[:], wqk.rearrange("(k p) o -> p k o", p=P)), (bqk_sb[:], bqk),
                             (wg_sb[:], wg.rearrange("(k p) o -> p k o", p=P)), (wout_sb[:], wout),
                             (vec_sb[:], vec), (ident_sb[:], ident)):
                sp.dma_start(dst, src).then_inc(weights_landed, 16)
            with sp.Fori(0, B) as b:
                with sp.Fori(0, CHUNKS // 2) as i:
                    for k in range(2):
                        sp.wait_ge(g_projected, b * CHUNKS + 2 * i + 1)
                        for kt in range(KT):
                            for copy in range(2):
                                sp.dma_start(x_ring[:, k, kt, :, copy], x[b, kt * P:(kt + 1) * P, bass.ts(
                                    2 * i + k, CHUNK)].rearrange("p (r w) -> p r w", w=W)).then_inc(x_landed[k], 16)
                with sp.Fori(0, GROUPS) as g:
                    sp.wait_ge(y_ready, b * GROUPS + g + 1)
                    sp.dma_start(x_res[:], x[b].rearrange("(k p) n -> p k n", p=P)[
                        :, :, bass.ts(g, QT * W)]).then_inc(res_landed, 16)
                    sp.wait_ge(y_ready, b * GROUPS + g + 2)
                    sp.dma_start(x1[b].rearrange("(k p) n -> p k n", p=P)[:, :, bass.ts(g, QT * W)],
                                 y[:]).then_inc(y_stored, 16)
            sp.wait_ge(y_stored, 16 * (B * GROUPS + 1))

        @block.tensor
        def _(pe):
            def score_max(n, t, kc, buf):
                pe.wait_ge(max_free, n + 1)
                qs, ks = bass.ts(t, P), bass.ts(kc, 512)
                nc.tensor.matmul(s_max[:, buf], q1[:, qs], kh[:, ks], start=True, stop=False)
                nc.tensor.matmul(s_max[:, buf], q2[:, qs], kl[:, ks], start=False, stop=True).then_inc(max_scored, 1)

            def score_t(grp, unit, g, u, buf, free):
                if free:
                    pe.wait_ge(probs_ready, unit - 1)
                qs = bass.ts(g, GROUP)
                for k in range(2):
                    ks = bass.ts(2 * u + k, P)
                    nc.tensor.matmul(sT[:, buf, k], kh[:, ks], q1[:, qs], start=True, stop=False)
                    last = nc.tensor.matmul(sT[:, buf, k], kl[:, ks], q2[:, qs], start=False, stop=True)
                last.then_inc(scored, 1)

            def weigh(unit, u, buf, first=False):
                pe.wait_ge(probs_ready, unit + 1)
                for k in range(2):
                    for t in range(QT):
                        last = nc.tensor.matmul(acc[:, t * (W + 1):(t + 1) * (W + 1)],
                                                probs[:, buf, k * GROUP + t * P:k * GROUP + (t + 1) * P],
                                                g_sb[:, 2 * u + k, :], start=first and k == 0 and t == 0,
                                                stop=False, skip_group_check=True)
                last.then_inc(pv_done, 1)

            def shift_rows(grp):
                pe.wait_ge(neg_ready, grp + 2)
                for t in range(QT):
                    last = nc.tensor.matmul(misc[:, t * P:(t + 1) * P], neg_max[:, t:t + 1].to_broadcast([P, P]),
                                            ident_sb[:], start=True, stop=True)
                last.then_inc(row_done, 1)

            def group(grp, g, ahead):
                n0 = (grp + 1) * MAXCH

                def look(c):
                    if ahead:
                        score_max(n0 + c, (g + 1) * QT + c % QT, c // QT, c % 2)

                pe.wait_ge(shift_ready, grp + 1)
                u0 = grp * UNITS
                score_t(grp, u0, g, 0, 0, False)
                score_t(grp, u0 + 1, g, 1, 1, False)
                pe.wait_ge(normed, grp + 1)
                weigh(u0, 0, 0, first=True)
                with pe.Fori(0, TURNS) as i:
                    for j in range(4):
                        u = 4 * i + 1 + j
                        score_t(grp, u0 + u + 1, g, u + 1, j % 2, True)
                        if ahead:
                            for c in (2 * j, 2 * j + 1):
                                score_max(n0 + 8 * i + c, (g + 1) * QT + c % QT, 2 * i + c // QT, c % 2)
                        weigh(u0 + u, u, (j + 1) % 2)
                for u in range(4 * TURNS + 1, UNITS):
                    if u + 1 < UNITS:
                        score_t(grp, u0 + u + 1, g, u + 1, (u + 1) % 2, True)
                        for k in range(4):
                            look(8 * TURNS + 4 * (u - 4 * TURNS - 1) + k)
                    elif ahead:
                        pe.wait_ge(y_ready, grp + 1)
                        shift_rows(grp + 1)
                    weigh(u0 + u, u, u % 2)
                if ahead:
                    pe.wait_ge(shift_ready, grp + 2)
                pe.wait_ge(normed, grp + 2)
                if not ahead:
                    pe.wait_ge(y_ready, grp + 1)
                for ct in range(KT):
                    last = nc.tensor.matmul(misc[:, ct * QT * W:(ct + 1) * QT * W], wout_sb[:, ct * P:(ct + 1) * P],
                                            o_grp[:], start=True, stop=True)
                last.then_inc(out_projected, 1)

            pe.wait_ge(weights_landed, 16 * LOADS)
            with pe.Fori(0, B) as b:
                with pe.Fori(0, CHUNKS // 2) as i:
                    for k in range(2):
                        chunk = b * CHUNKS + 2 * i + k
                        pe.wait_ge(x_landed[k], 64 * (b * (CHUNKS // 2) + i) + 64)
                        for hh in range(ROWS // 2):
                            if hh >= 2:
                                pe.wait_ge(qk_biased, chunk * 4 + hh)
                            else:
                                pe.wait_ge(qk_biased, chunk * 4 + 1)
                            for j in range(2):
                                row = 2 * hh + j
                                for kt in range(KT):
                                    xs = x_ring[:, k, kt, row].rearrange("p c w -> p (c w)")
                                    last = nc.tensor.matmul(sT[:, hh % 2, 0, j * 2 * CH:(j + 1) * 2 * CH], xs,
                                                            wqk_sb[:, kt], start=kt == 0, stop=kt == KT - 1)
                            last.then_inc(qk_projected, 1)
                        pe.wait_ge(g_ready, chunk + 1)
                        if k == 0:
                            pe.wait_ge(y_ready, b * GROUPS + 1)
                        for kt in range(KT):
                            last = nc.tensor.matmul(misc[:], wg_sb[:, kt], x_ring[:, k, kt, :, 0], start=kt == 0,
                                                    stop=kt == KT - 1)
                        last.then_inc(g_projected, 1)
                with pe.Fori(0, MAXCH // 8) as i:
                    pe.wait_ge(split_done, (b + 1) * CHUNKS * 4 + 1)
                    for c in range(8):
                        score_max(b * GROUPS * MAXCH + 8 * i + c, c % QT, 2 * i + c // QT, c % 2)
                pe.wait_ge(g_ready, (b + 1) * CHUNKS + 1)
                shift_rows(b * GROUPS)
                with pe.Fori(0, GROUPS - 1) as g:
                    group(b * GROUPS + g, g, True)
                group(b * GROUPS + GROUPS - 1, GROUPS - 1, False)

        @block.scalar
        def _(act):
            act.wait_ge(weights_landed, 16 * LOADS)

            def exponent(unit, buf, free):
                act.wait_ge(scored, unit + 1)
                if free:
                    act.wait_ge(pv_done, unit - 1)
                nc.scalar.activation(probs[:, buf], sT[:, buf].rearrange("p k n -> p (k n)"),
                                     ACT.Exp).then_inc(probs_ready, 1)

            with act.Fori(0, B) as b:
                with act.Fori(0, CHUNKS) as c:
                    chunk = b * CHUNKS + c
                    for hh in range(ROWS // 2):
                        act.wait_ge(qk_biased, chunk * 4 + hh + 2)
                        pr = proj[:, hh % 2]
                        cols = bass.ds(c * ROWS * CH + hh * 2 * CH, 2 * CH)

                        def two(t, lo=0, hi=P):
                            return t[lo:hi, cols].rearrange("p (r o) -> p r o", r=2)
                        nc.scalar.copy(two(q1), pr[:, :, 0:CH])
                        nc.scalar.copy(two(kh), pr[:, :, CH:2 * CH])
                        nc.scalar.copy(two(q2, 0, HALF), pr[0:HALF, :, 0:CH]).then_inc(high_done, 1)
                    act.wait_ge(g_projected, chunk + 2)
                    nc.scalar.activation(g_sb[:, bass.ts(c, ROWS), 0:W], misc[:].rearrange("p (r w) -> p r w", w=W),
                                         ACT.Identity, bias=vec_sb[:, VEC["b_g"]:VEC["b_g"] + 1]).then_inc(g_ready, 1)
                with act.Fori(0, GROUPS) as g:
                    u0 = (b * GROUPS + g) * UNITS
                    exponent(u0, 0, False)
                    exponent(u0 + 1, 1, False)
                    with act.Fori(0, UNITS // 2 - 1) as i:
                        for k in range(2):
                            exponent(u0 + 2 * i + 2 + k, k, True)

        @block.gpsimd
        def _(pool):
            for s in (qk_biased, split_done, g_ready, g_projected, normed, neg_ready, y_ready):
                pool.sem_inc(s, 1)
            pool.sem_inc(y_stored, 16)

        @block.vector
        def _(dve):
            def negate(grp):
                dve.wait_ge(max_free, 2 + (grp + 1) * MAXCH)
                dve.wait_ge(neg_ready, grp + 1)
                nc.vector.tensor_reduce(qmax[:], chunk_max[:].rearrange("p k t -> p t k"), X, ALU.max).then_inc(qmax_done, 1)
                dve.wait_ge(qmax_done, grp + 1)
                nc.vector.tensor_scalar(neg_max[:], qmax[:], -1.0, None, ALU.mult).then_inc(neg_ready, 1)

            def write_shift(grp, g):
                cols = bass.ts(g, GROUP)
                dve.wait_ge(row_done, grp + 1)
                nc.vector.tensor_copy(q2[HALF:P, cols], misc[HALF:P, :]).then_inc(row_high, 1)
                dve.wait_ge(row_high, grp + 1)
                nc.vector.tensor_tensor(q2[HALF + 32:P, cols], misc[HALF + 32:P, :], q2[HALF + 32:P, cols],
                                        ALU.subtract).then_inc(shift_ready, 1)

            def group(grp, g, ahead):
                n0 = (grp + 1) * MAXCH
                if ahead:
                    with dve.Fori(0, MAXCH // 2) as i:
                        for k in range(2):
                            c = 2 * i + k
                            dve.wait_ge(max_scored, n0 + c + 1)
                            nc.vector.tensor_reduce(chunk_max_flat[:, bass.ds(c, 1)], s_max[:, k], X,
                                                    ALU.max).then_inc(max_free, 1)
                    negate(grp + 1)
                    write_shift(grp + 1, g + 1)
                dve.wait_ge(pv_done, (grp + 1) * UNITS)
                outs = acc[:, 0:QT * (W + 1)].rearrange("p (t w) -> p t w", t=QT)
                nc.vector.reciprocal(rden[:].unsqueeze(2), outs[:, :, W:W + 1]).then_inc(rden_done, 1)
                dve.wait_ge(rden_done, grp + 1)
                nc.vector.tensor_tensor(o_grp[:].rearrange("p (t w) -> p t w", t=QT), outs[:, :, 0:W],
                                        rden[:].unsqueeze(2).to_broadcast([P, QT, W]), ALU.mult).then_inc(normed, 1)
                dve.wait_ge(out_projected, grp + 1)
                dve.wait_ge(res_landed, 16 * (grp + 1))
                dve.wait_ge(y_stored, 16 * grp + 16)
                for ct in range(KT):
                    last = nc.vector.scalar_tensor_tensor(
                        y[:, ct], misc[:, ct * QT * W:(ct + 1) * QT * W],
                        vec_sb[:, VEC["b_out"] + ct:VEC["b_out"] + ct + 1], x_res[:, ct], ALU.add, ALU.add)
                last.then_inc(y_ready, 1)

            chunk_max_flat = chunk_max[:].rearrange("p k t -> p (k t)")
            dve.wait_ge(weights_landed, 16 * LOADS)
            nc.vector.memset(chunk_max[:, 0], 0.0).then_inc(max_free, 1)
            nc.vector.memset(chunk_max[:, 1], 0.0).then_inc(max_free, 1)
            nc.vector.memset(g_sb[:, :, W:W + 1], 1.0)
            nc.vector.memset(kl[HALF:P, :].bitcast(F32), 0.0).then_inc(kl_zeroed, 1)
            dve.wait_ge(kl_zeroed, 1)
            nc.vector.memset(kl[HALF:HALF + 1, :], 1.0)
            nc.vector.memset(kl[HALF + 32:HALF + 33, :], 1.0)
            with dve.Fori(0, B) as b:
                nc.vector.memset(q2[HALF:P, :].bitcast(F32), 0.0)
                with dve.Fori(0, CHUNKS) as c:
                    chunk = b * CHUNKS + c

                    def bias(hh):
                        dve.wait_ge(split_done, chunk * 4 + (hh if hh >= 2 else 1))
                        dve.wait_ge(qk_projected, chunk * 4 + hh + 1)
                        nc.vector.tensor_tensor(proj[:, hh % 2], sT[:, hh % 2, 0].rearrange("p (r o) -> p r o", r=2),
                                                bqk_sb[:].unsqueeze(1).to_broadcast([P, 2, 2 * CH]),
                                                ALU.add).then_inc(qk_biased, 1)

                    def low(hh):
                        dve.wait_ge(high_done, chunk * 4 + hh + 1)
                        cols = bass.ds(c * ROWS * CH + hh * 2 * CH, 2 * CH)
                        pr = proj[:, hh % 2]
                        ql = q1[HALF:P, cols].rearrange("p (r o) -> p r o", r=2)
                        nc.vector.tensor_tensor(ql, pr[HALF:P, :, 0:CH], ql, ALU.subtract)
                        nc.vector.tensor_tensor(kl[0:HALF, cols].rearrange("p (r o) -> p r o", r=2),
                                                pr[0:HALF, :, CH:2 * CH],
                                                kh[0:HALF, cols].rearrange("p (r o) -> p r o", r=2),
                                                ALU.subtract).then_inc(split_done, 1)
                    bias(0)
                    bias(1)
                    low(0)
                    bias(2)
                    low(1)
                    bias(3)
                    low(2)
                    low(3)
                with dve.Fori(0, MAXCH // 2) as i:
                    for k in range(2):
                        c = 2 * i + k
                        dve.wait_ge(max_scored, b * GROUPS * MAXCH + c + 1)
                        nc.vector.tensor_reduce(chunk_max_flat[:, bass.ds(c, 1)], s_max[:, k], X,
                                                ALU.max).then_inc(max_free, 1)
                negate(b * GROUPS)
                write_shift(b * GROUPS, 0)
                with dve.Fori(0, GROUPS - 1) as g:
                    group(b * GROUPS + g, g, True)
                group(b * GROUPS + GROUPS - 1, GROUPS - 1, False)


def swin_part(nc, x1, qkvw, bv, rpb, projw, gaze, fc1w, fc2w, vec, ident, out):
    with ExitStack() as ctx:
        def sb(name, shape, dt=F32):
            return ctx.enter_context(nc.sbuf_tensor(name, shape, dt))

        def sem(name):
            return ctx.enter_context(nc.semaphore(name))

        qkvw_sb = sb("qkvw_sb", [P, KT, 3 * C])
        bv_sb = sb("bv_sb", [P, C])
        rpb_sb = sb("rpb_sb", [P, HP * WS * WS])
        projw_sb = sb("projw_sb", [P, KT, C])
        gaze_sb = sb("gaze_sb", [P, KT, GK * GK])
        fc1w_sb = sb("fc1w_sb", [P, KT, HID])
        fc2w_sb = sb("fc2w_sb", [P, FT, C])
        vec_sb = sb("vec_sb2", [P, NVEC])
        ident_sb = sb("ident_sb2", [P, P])
        mean_w = sb("mean_w", [P, P])
        eps = sb("eps", [P, 1])
        x_in = sb("x_in", [P, 2, KT, CHUNK])
        xc = sb("xc", [P, KT, CHUNK])
        sq = sb("sq", [P, KT, CHUNK])
        std = sb("std", [P, CHUNK])
        rstd = sb("rstd", [P, CHUNK])
        xh = sb("xh", [P, KT, CHUNK])
        xn = sb("xn", [P, KT, CHUNK])
        qm = sb("qm", [P, KT, 2, W // WS, 2, WS * WS])
        qb4 = sb("qb4", [P, KT])
        k_sb = sb("k_sb", [P, KT, CHUNK])
        vt = sb("vt", [P, 4, C])
        att = sb("att", [P, 2, CHUNK])
        amax = sb("amax", [P, 2, NH])
        den = sb("den", [P, 2, NH])
        rden = sb("rden2", [P, 2, NH])
        attT = sb("attT", [P, 2, CHUNK])
        vimg = sb("vimg", [P, KT, PADW, PADW])
        osum = sb("osum", [P, KT, PIX])
        x2 = sb("x2", [P, KT, CHUNK])
        hid = sb("hid", [P, FT, CHUNK])
        y = sb("y2", [P, KT, CHUNK])

        def bank(name):
            return ctx.enter_context(nc.psum_tensor(name, [P, 512], F32))

        pj = [bank("pj0"), bank("pj1")]
        sc = [bank("sc0"), bank("sc1")]
        tp = [bank("tp0"), bank("tp1")]
        ob = [bank("ob0"), bank("ob1")]

        weights_landed = sem("weights_landed2")
        setup_done = sem("setup_done")
        padding_done = sem("padding_done")
        x_landed = [sem("xin_landed0"), sem("xin_landed1")]
        mean_done = sem("mean_done")
        centered = sem("centered")
        squared = sem("squared")
        var_done = sem("var_done")
        std_done = sem("std_done")
        rstd_done = sem("rstd_done")
        scaled = sem("scaled")
        xn_ready = sem("xn_ready")
        projected = sem("projected")
        q_ready = [sem("q_ready0"), sem("q_ready1")]
        k_ready = [sem("k_ready0"), sem("k_ready1")]
        vi_ready = [sem("vi_ready0"), sem("vi_ready1")]
        vt_ready = sem("vt_ready")
        att_scored = sem("att_scored")
        att_biased = sem("att_biased")
        amax_done = sem("amax_done")
        shifted = sem("shifted")
        exped = sem("exped")
        den_done = sem("den_done")
        rden_done = sem("rden_done2")
        att_ready = sem("att_ready")
        transposed = sem("transposed")
        attT_ready = sem("attT_ready")
        weighing = sem("weighing")
        attended = sem("attended")
        o_copied = sem("o_copied")
        tapped = sem("tapped")
        out_projected = sem("out_projected2")
        x2_ready = sem("x2_ready")
        fc1_done = sem("fc1_done")
        hid_ready = sem("hid_ready")
        fc2_done = sem("fc2_done")
        y_ready = sem("y_ready2")
        y_stored = sem("y_stored2")

        LOADS = 9
        NTAP = GK * GK
        PAIRS = 4
        SLOTS = 8

        def v(name, kt=0):
            return vec_sb[:, VEC[name] + kt:VEC[name] + kt + 1]

        def win(t):
            return t.rearrange("p (c r s) -> p r c s", c=W // WS, r=WS)

        def qm_head(rows, kt, r):
            return qm[rows, kt, r // 2, :, r % 2, :]

        def v_rows(kt, i):
            return vimg[:, kt, GK // 2:GK // 2 + H, GK // 2:GK // 2 + W].rearrange(
                "p (r i) (s c) -> p i c r s", i=WS, c=WS)[:, bass.ds(i, 1)].squeeze(1)

        def o_rows(kt, i):
            return osum[:, kt].rearrange("p (r i s c) -> p i c r s", r=WS, i=WS, s=WS)[:, bass.ds(i, 1)].squeeze(1)

        block = ctx.enter_context(nc.Block())

        @block.sync
        def _(sp):
            for dst, src in ((qkvw_sb[:], qkvw.rearrange("(k p) o -> p k o", p=P)), (bv_sb[:], bv), (rpb_sb[:], rpb),
                             (projw_sb[:], projw.rearrange("(k p) o -> p k o", p=P)), (gaze_sb[:], gaze),
                             (fc1w_sb[:], fc1w.rearrange("(k p) o -> p k o", p=P)),
                             (fc2w_sb[:], fc2w.rearrange("(k p) o -> p k o", p=P)),
                             (vec_sb[:], vec), (ident_sb[:], ident)):
                sp.dma_start(dst, src).then_inc(weights_landed, 16)

            def load(b, i, k):
                sp.dma_start(x_in[:, k], x1[b].rearrange("(k p) n -> p k n", p=P)[
                    :, :, bass.ts(i, CHUNK)]).then_inc(x_landed[k], 16)

            with sp.Fori(0, B) as b:
                with sp.Fori(0, CHUNKS // 2) as i:
                    for k in range(2):
                        sp.wait_ge(centered, b * 2 * CHUNKS + 2 * i + 1)
                        load(b, 2 * i + k, k)
                with sp.Fori(0, CHUNKS // 2) as i:
                    for k in range(2):
                        n = b * CHUNKS + 2 * i + k
                        if k == 0:
                            sp.wait_ge(x2_ready, b * CHUNKS + 2 * i + 1)
                            sp.wait_ge(centered, (b * 2 + 1) * CHUNKS + 1)
                            load(b, 2 * i, 0)
                            load(b, 2 * i + 1, 1)
                        sp.wait_ge(y_ready, n + 2)
                        sp.dma_start(out[b].rearrange("(k p) n -> p k n", p=P)[:, :, bass.ts(2 * i + k, CHUNK)],
                                     y[:]).then_inc(y_stored, 16)
            sp.wait_ge(y_stored, 16 * (B * CHUNKS + 1))

        @block.gpsimd
        def _(pool):
            for s in (centered, scaled, xn_ready, vt_ready, vt_ready, o_copied, x2_ready, y_ready, fc2_done,
                      att_biased, att_biased, transposed, transposed, attT_ready, attT_ready, attended, attended,
                      tapped, tapped, hid_ready, hid_ready):
                pool.sem_inc(s, 1)
            pool.sem_inc(y_stored, 16)
            with pool.Fori(0, B * CHUNKS) as it:
                def subtract(p):
                    pool.wait_ge(amax_done, it * PAIRS + p + 1)
                    a = att[:, p % 2].rearrange("p (g m) -> p g m", g=NH)
                    nc.gpsimd.tensor_tensor(a, a, amax[:, p % 2].unsqueeze(2).to_broadcast([P, NH, WS * WS]),
                                            ALU.subtract).then_inc(shifted, 1)

                def normalise(p):
                    pool.wait_ge(rden_done, it * PAIRS + p + 1)
                    a = att[:, p % 2].rearrange("p (g m) -> p g m", g=NH)
                    nc.gpsimd.tensor_tensor(a, a, rden[:, p % 2].unsqueeze(2).to_broadcast([P, NH, WS * WS]),
                                            ALU.mult).then_inc(att_ready, 1)
                subtract(0)
                for p in range(1, PAIRS):
                    subtract(p)
                    normalise(p - 1)
                normalise(PAIRS - 1)

        @block.tensor
        def _(pe):
            def norm(n, src, landed):
                landed()
                pe.wait_ge(centered, n + 1)
                for kt in range(KT):
                    last = nc.tensor.matmul(pj[0][:], mean_w[:], src(kt), start=kt == 0, stop=kt == KT - 1)
                last.then_inc(mean_done, 1)
                pe.wait_ge(squared, n + 1)
                for kt in range(KT):
                    last = nc.tensor.matmul(pj[1][:], mean_w[:], sq[:, kt], start=kt == 0, stop=kt == KT - 1)
                last.then_inc(var_done, 1)

            def qkv(it, n):
                def project(bank, col):
                    for kt in range(KT):
                        last = nc.tensor.matmul(bank[:], qkvw_sb[:, kt, col:col + P], xn[:, kt],
                                                start=kt == 0, stop=kt == KT - 1)
                    last.then_inc(projected, 1)
                pe.wait_ge(xn_ready, n + 2)
                for ct in range(KT):
                    project(pj[ct], ct * P)
                for ct in range(KT):
                    pe.wait_ge(q_ready[ct], it + 1)
                    project(pj[ct], C + ct * P)
                for ct in range(KT):
                    pe.wait_ge(k_ready[ct], it + 1)
                    project(pj[ct], 2 * C + ct * P)
                for h in range(2):
                    pe.wait_ge(vi_ready[h], it + 1)
                    for p in range(2):
                        t = (2 * h + p) * P
                        for kt in range(KT):
                            last = nc.tensor.matmul(pj[h][:, p * C:(p + 1) * C], xn[:, kt, t:t + P],
                                                    qkvw_sb[:, kt, 2 * C:3 * C], start=kt == 0, stop=kt == KT - 1)
                    last.then_inc(projected, 1)

            def scores(wp, p):
                pe.wait_ge(att_biased, wp + 1)
                for w in range(2):
                    t = p * P + w * WS * WS
                    for hp in range(HP):
                        lhsT = qm[:, hp // 2, hp % 2, 2 * p + w].rearrange("p b t -> p (b t)")
                        last = nc.tensor.matmul(sc[p % 2][:, (2 * hp + w) * 64:(2 * hp + w + 1) * 64], lhsT,
                                                k_sb[:, hp // 2, t:t + WS * WS], start=True, stop=True)
                last.then_inc(att_scored, 1)

            def turn(wp, p):
                pe.wait_ge(att_ready, wp + 1)
                pe.wait_ge(attT_ready, wp + 1)
                for hp in range(HP):
                    last = nc.tensor.transpose(tp[p % 2][:, hp * P:(hp + 1) * P], att[:, p % 2, hp * P:(hp + 1) * P], ident_sb[:])
                last.then_inc(transposed, 1)

            def weigh(it, wp, p):
                pe.wait_ge(attT_ready, wp + 3)
                if p == 0:
                    pe.wait_ge(o_copied, it + 1)
                pe.sem_inc(weighing, 1)
                for w in range(2):
                    for h in range(NH):
                        r = h % 4
                        col = (p * KT + h // 4) * 64
                        last = nc.tensor.matmul(ob[w][32 * r:32 * r + 32, col:col + 64],
                                                vt[64 * w:64 * w + 64, p, h * HD:(h + 1) * HD],
                                                attT[64 * w:64 * w + 64, p % 2, h * 64:(h + 1) * 64],
                                                start=True, stop=True)
                last.then_inc(attended, 1)

            pe.wait_ge(weights_landed, 16 * LOADS)
            pe.wait_ge(setup_done, 3)
            with pe.Fori(0, B) as b:
                with pe.Fori(0, CHUNKS // 2) as i:
                    for k in range(2):
                        it = b * CHUNKS + 2 * i + k
                        n = b * 2 * CHUNKS + 2 * i + k

                        def landed():
                            pe.wait_ge(x_landed[k], 16 * (b * CHUNKS + i + 1))
                            pe.wait_ge(vt_ready, it * 2 + 2)
                        norm(n, lambda kt: x_in[:, k, kt], landed)
                        qkv(it, n)
                        pe.wait_ge(q_ready[1], it + 1)
                        pe.wait_ge(k_ready[1], it + 1)
                        pe.wait_ge(k_ready[0], it + 1)
                        wp = it * PAIRS
                        scores(wp, 0)
                        scores(wp + 1, 1)
                        pe.wait_ge(vt_ready, it * 2 + 4)
                        for p in range(PAIRS):
                            if p + 2 < PAIRS:
                                scores(wp + p + 2, p + 2)
                            turn(wp + p, p)
                            if p:
                                weigh(it, wp + p - 1, p - 1)
                        weigh(it, wp + PAIRS - 1, PAIRS - 1)
                with pe.Fori(0, CHUNKS // 2) as i:
                    for k in range(2):
                        it = b * CHUNKS + 2 * i + k
                        n = (b * 2 + 1) * CHUNKS + 2 * i + k
                        pe.wait_ge(tapped, (b + 1) * NTAP * KT + 2)
                        pe.wait_ge(vt_ready, (b + 1) * CHUNKS * 2 + 2)
                        pe.wait_ge(y_ready, it + 1)
                        for ct in range(KT):
                            for kt in range(KT):
                                last = nc.tensor.matmul(pj[ct][:], projw_sb[:, kt, ct * P:(ct + 1) * P],
                                                        o_rows(kt, 2 * i + k).rearrange("p c r s -> p r c s"), start=kt == 0,
                                                        stop=kt == KT - 1)
                        last.then_inc(out_projected, 1)
                        norm(n, lambda kt: x2[:, kt], lambda: pe.wait_ge(x2_ready, it + 2))
                        pe.wait_ge(xn_ready, n + 2)
                        banks = sc + tp

                        def fc1(ft):
                            if ft >= 4:
                                pe.wait_ge(hid_ready, it * FT + ft - 1)
                            for kt in range(KT):
                                last = nc.tensor.matmul(banks[ft % 4][:], fc1w_sb[:, kt, ft * P:(ft + 1) * P],
                                                        xn[:, kt], start=kt == 0, stop=kt == KT - 1)
                            last.then_inc(fc1_done, 1)

                        def fc2(ft):
                            pe.wait_ge(hid_ready, it * FT + ft + 3)
                            for ct in range(KT):
                                last = nc.tensor.matmul(ob[ct][:], fc2w_sb[:, ft, ct * P:(ct + 1) * P], hid[:, ft],
                                                        start=ft == 0, stop=ft == FT - 1)
                            if ft == FT - 1:
                                last.then_inc(fc2_done, 1)
                        for ft in range(FT):
                            fc1(ft)
                            if ft >= 2:
                                fc2(ft - 2)
                        fc2(FT - 2)
                        fc2(FT - 1)

        @block.scalar
        def _(act):
            act.wait_ge(weights_landed, 16 * LOADS)
            act.wait_ge(setup_done, 3)

            def norm(n, dst):
                act.wait_ge(centered, n + 2)
                nc.scalar.activation(sq[:], xc[:], ACT.Square).then_inc(squared, 1)
                act.wait_ge(var_done, n + 1)
                nc.scalar.activation(std[:], pj[1][:], ACT.Sqrt, bias=eps[:]).then_inc(std_done, 1)
                act.wait_ge(scaled, n + 2)
                dst()

            def affine(g, bias, order):
                for kt in range(KT):
                    src = xh[:, kt]
                    dst = xn[:, kt]
                    if order:
                        src, dst = src.rearrange("p (r c s) -> p r c s", r=WS, s=WS), win(dst)
                    last = nc.scalar.activation(dst, src, ACT.Identity, scale=v(g, kt), bias=v(bias, kt))
                last.then_inc(xn_ready, 1)

            with act.Fori(0, B) as b:
                with act.Fori(0, CHUNKS) as i:
                    it = b * CHUNKS + i
                    n = b * 2 * CHUNKS + i
                    norm(n, lambda: affine("norm1_g", "norm1_b", True))
                    act.wait_ge(projected, it * SLOTS + 1)
                    for r in range(4):
                        rows = slice(32 * r, 32 * r + 32)
                        last = nc.scalar.activation(qm_head(rows, 0, r), pj[0][rows, :].rearrange(
                            "p (c t) -> p c t", c=WS), ACT.Identity, scale=SCALE, bias=qb4[rows, 0:1])
                    last.then_inc(q_ready[0], 1)
                    act.wait_ge(projected, it * SLOTS + 3)
                    nc.scalar.activation(k_sb[:, 0], pj[0][:], ACT.Identity, bias=v("qkv_b", 2)).then_inc(k_ready[0], 1)
                    act.wait_ge(projected, it * SLOTS + 5)
                    act.wait_ge(tapped, b * NTAP * KT + 2)
                    nc.scalar.activation(v_rows(0, i), pj[0][:].rearrange("p (c r s) -> p c r s", c=WS, r=WS),
                                         ACT.Identity, bias=v("qkv_b", 4)).then_inc(vi_ready[0], 1)

                    def exponent(p):
                        act.wait_ge(shifted, it * PAIRS + p + 1)
                        nc.scalar.activation(att[:, p % 2], att[:, p % 2], ACT.Exp).then_inc(exped, 1)

                    def copy_turned(p):
                        act.wait_ge(transposed, it * PAIRS + p + 3)
                        act.wait_ge(attended, it * PAIRS + p + 1)
                        nc.scalar.copy(attT[:, p % 2], tp[p % 2][:]).then_inc(attT_ready, 1)
                    exponent(0)
                    exponent(1)
                    for p in range(PAIRS):
                        copy_turned(p)
                        if p + 2 < PAIRS:
                            exponent(p + 2)
                    act.wait_ge(attended, (it + 1) * PAIRS + 2)
                    for w in range(2):
                        for kt in range(KT):
                            src = ob[w][:].rearrange("p (q k r s) -> p k q r s", k=KT, r=WS, s=WS)[:, kt]
                            dst = o_rows(kt, i).rearrange("p (q w) r s -> p w q r s", w=2)[:, w]
                            last = nc.scalar.activation(dst, src, ACT.Identity, bias=v("gaze_b", kt))
                    last.then_inc(o_copied, 1)
                with act.Fori(0, CHUNKS) as i:
                    it = b * CHUNKS + i
                    norm((b * 2 + 1) * CHUNKS + i, lambda: affine("norm2_g", "norm2_b", False))
                    for ft in range(FT):
                        act.wait_ge(fc1_done, it * FT + ft + 1)
                        if ft == 0:
                            act.wait_ge(fc2_done, it + 1)
                        nc.scalar.activation(hid[:, ft], (sc + tp)[ft % 4][:], ACT.Gelu,
                                             bias=v("fc1_b", ft)).then_inc(hid_ready, 1)

        @block.vector
        def _(dve):
            nc.vector.memset(mean_w[:], 1.0 / C)
            nc.vector.memset(eps[:], EPS).then_inc(setup_done, 1)
            nc.vector.memset(qm[:], 0.0).then_inc(setup_done, 1)
            nc.vector.memset(vimg[:], 0.0).then_inc(padding_done, 1)
            dve.wait_ge(weights_landed, 16 * LOADS)
            nc.vector.tensor_scalar(qb4[:], vec_sb[:, VEC["qkv_b"]:VEC["qkv_b"] + KT], SCALE, None,
                                    ALU.mult).then_inc(setup_done, 1)
            dve.wait_ge(setup_done, 3)
            dve.wait_ge(padding_done, 1)

            def norm(n, src):
                dve.wait_ge(mean_done, n + 1)
                dve.wait_ge(scaled, n + 1)
                for kt in range(KT):
                    last = nc.vector.tensor_tensor(xc[:, kt], src(kt), pj[0][:], ALU.subtract)
                last.then_inc(centered, 1)
                dve.wait_ge(std_done, n + 1)
                nc.vector.reciprocal(rstd[:], std[:]).then_inc(rstd_done, 1)
                dve.wait_ge(rstd_done, n + 1)
                dve.wait_ge(xn_ready, n + 1)
                for kt in range(KT):
                    last = nc.vector.tensor_tensor(xh[:, kt], xc[:, kt], rstd[:], ALU.mult)
                last.then_inc(scaled, 1)

            with dve.Fori(0, B) as b:
                with dve.Fori(0, CHUNKS // 2) as i:
                    for k in range(2):
                        it = b * CHUNKS + 2 * i + k
                        norm(b * 2 * CHUNKS + 2 * i + k, lambda kt: x_in[:, k, kt])
                        dve.wait_ge(projected, it * SLOTS + 2)
                        for r in range(4):
                            rows = slice(32 * r, 32 * r + 32)
                            last = nc.vector.tensor_scalar(qm_head(rows, 1, r), pj[1][rows, :].rearrange(
                                "p (c t) -> p c t", c=WS), SCALE, qb4[rows, 1:2], ALU.mult, ALU.add)
                        last.then_inc(q_ready[1], 1)
                        dve.wait_ge(projected, it * SLOTS + 4)
                        nc.vector.tensor_scalar(k_sb[:, 1], pj[1][:], v("qkv_b", 3), None, ALU.add).then_inc(k_ready[1], 1)
                        dve.wait_ge(projected, it * SLOTS + 6)
                        dve.wait_ge(tapped, b * NTAP * KT + 2)
                        nc.vector.tensor_scalar(v_rows(1, 2 * i + k), pj[1][:].rearrange(
                            "p (c r s) -> p c r s", c=WS, r=WS), v("qkv_b", 5), None, ALU.add).then_inc(vi_ready[1], 1)
                        for h in range(2):
                            dve.wait_ge(projected, it * SLOTS + 7 + h)
                            if h == 0:
                                dve.wait_ge(attended, it * PAIRS + 2)
                            nc.vector.tensor_tensor(vt[:, 2 * h:2 * h + 2], pj[h][:].rearrange("p (q c) -> p q c", q=2),
                                                    bv_sb[:].unsqueeze(1).to_broadcast([P, 2, C]),
                                                    ALU.add).then_inc(vt_ready, 1)

                        def bias_and_max(p):
                            wp = it * PAIRS + p
                            dve.wait_ge(att_scored, wp + 1)
                            dve.wait_ge(transposed, wp + 1)
                            def by_window(a):
                                return a.rearrange("p (h w m) -> p h w m", h=HP, w=2)
                            nc.vector.tensor_tensor(by_window(att[:, p % 2]), by_window(sc[p % 2][:]),
                                                    rpb_sb[:].rearrange("p (h m) -> p h m", h=HP).unsqueeze(2)
                                                    .to_broadcast([P, HP, 2, WS * WS]),
                                                    ALU.add).then_inc(att_biased, 1)
                            dve.wait_ge(att_biased, wp + 3)
                            nc.vector.tensor_reduce(amax[:, p % 2], att[:, p % 2].rearrange("p (g m) -> p g m", g=NH),
                                                    X, ALU.max).then_inc(amax_done, 1)

                        def denominators(p):
                            wp = it * PAIRS + p
                            dve.wait_ge(exped, wp + 1)
                            nc.vector.tensor_reduce(den[:, p % 2], att[:, p % 2].rearrange("p (g m) -> p g m", g=NH),
                                                    X, ALU.add).then_inc(den_done, 1)
                            dve.wait_ge(den_done, wp + 1)
                            nc.vector.reciprocal(rden[:, p % 2], den[:, p % 2]).then_inc(rden_done, 1)
                        bias_and_max(0)
                        bias_and_max(1)
                        for p in range(PAIRS):
                            denominators(p)
                            if p + 2 < PAIRS:
                                bias_and_max(p + 2)
                with dve.Fori(0, GK) as dh:
                    with dve.Fori(0, GK) as dw:
                        for kt in range(KT):
                            tap = (b * NTAP + dh * GK + dw) * KT + kt
                            dve.wait_ge(o_copied, (b + 1) * CHUNKS + 1)
                            dve.wait_ge(tapped, tap + 1)
                            o = osum[:, kt].rearrange("p (r w) -> p r w", w=W)
                            nc.vector.scalar_tensor_tensor(o, vimg[:, kt, bass.ds(dh, H), bass.ds(dw, W)],
                                                           gaze_sb[:, kt, bass.ds(dh * GK + dw, 1)], o,
                                                           ALU.mult, ALU.add).then_inc(tapped, 1)
                with dve.Fori(0, CHUNKS // 2) as i:
                    for k in range(2):
                        it = b * CHUNKS + 2 * i + k
                        dve.wait_ge(out_projected, it + 1)
                        dve.wait_ge(x_landed[k], 16 * (b * CHUNKS + CHUNKS // 2 + i + 1))
                        for ct in range(KT):
                            last = nc.vector.scalar_tensor_tensor(x2[:, ct], pj[ct][:], v("proj_b", ct), x_in[:, k, ct],
                                                                  ALU.add, ALU.add)
                        last.then_inc(x2_ready, 1)
                        norm((b * 2 + 1) * CHUNKS + 2 * i + k, lambda kt: x2[:, kt])
                        dve.wait_ge(fc2_done, it + 2)
                        dve.wait_ge(y_stored, 16 * it + 16)
                        for ct in range(KT):
                            last = nc.vector.scalar_tensor_tensor(y[:, ct], ob[ct][:], v("fc2_b", ct), x2[:, ct],
                                                                  ALU.add, ALU.add)
                        last.then_inc(y_ready, 1)


def program(nc, x, wqk, bqk, wg, wout, vec, ident, qkvw, bv, rpb, projw, gaze, fc1w, fc2w, out):
    x1 = nc.dram_tensor("x1_scratch", (B, C, PIX), F32).ap()
    nonlocal_part(nc, x, wqk, bqk, wg, wout, vec, ident, x1)
    swin_part(nc, x1, qkvw, bv, rpb, projw, gaze, fc1w, fc2w, vec, ident, out)


def kernel(**inputs):
    import numpy as np
    import concourse.bacc as bacc
    from concourse.bass_utils import run_bass_kernel_spmd

    a = {k: np.asarray(v) for k, v in inputs.items()}
    L0, L1 = "L0_conv_", "L1_conv_"

    def cols(v):
        return v.reshape(-1, P).T

    vec = np.concatenate([cols(v) for v in (
        a[L0 + "b_g"], a[L0 + "b_out"], a[L1 + "norm1_g"], a[L1 + "norm1_b"], a[L1 + "qkv_b"], a[L1 + "proj_b"],
        a[L1 + "gaze_b"], a[L1 + "norm2_g"], a[L1 + "norm2_b"], a[L1 + "fc1_b"], a[L1 + "fc2_b"])], axis=1)
    at = np.stack(np.meshgrid(np.arange(WS), np.arange(WS), indexing="ij")).reshape(2, -1)
    off = at[:, :, None] - at[:, None, :] + WS - 1
    rpb = a[L1 + "rpb_table"][off[0] * (2 * WS - 1) + off[1]]
    rpb = rpb.reshape(WS * WS, WS * WS, HP, 2).transpose(3, 0, 2, 1).reshape(P, HP * WS * WS)
    arrays = {
        "x": a["x"].reshape(B, C, PIX),
        "wqk": np.concatenate([a[L0 + "w_theta"], a[L0 + "w_phi"]]).T,
        "bqk": np.broadcast_to(np.concatenate([a[L0 + "b_theta"], a[L0 + "b_phi"]]), (P, 2 * CH)),
        "wg": a[L0 + "w_g"].T,
        "wout": a[L0 + "w_out"].T,
        "vec": vec,
        "ident": np.eye(P, dtype=np.float32),
        "qkvw": a[L1 + "qkv_w"].T,
        "bv": np.broadcast_to(a[L1 + "qkv_b"][2 * C:], (P, C)),
        "rpb": rpb,
        "projw": a[L1 + "proj_w"].T,
        "gaze": a[L1 + "gaze_w"].reshape(GK * GK, KT, P).transpose(2, 1, 0),
        "fc1w": a[L1 + "fc1_w"].T,
        "fc2w": a[L1 + "fc2_w"].T,
    }
    nc = bacc.Bacc("TRN2", target_bir_lowering=False, num_devices=1)
    fed, args = {}, []
    for name, v in arrays.items():
        v = np.ascontiguousarray(v)
        fed[f"in_{name}"] = v
        args.append(nc.dram_tensor(f"in_{name}", v.shape, mybir.dt.from_np(v.dtype), kind="ExternalInput").ap())
    args.append(nc.dram_tensor("out_x", (B, C, PIX), F32, kind="ExternalOutput").ap())
    program(nc, *args)
    r = run_bass_kernel_spmd(nc, [fed], core_ids=[0])
    return r.results[0]["out_x"].reshape(B, C, H, W)
```

```python
from contextlib import ExitStack

import concourse.bass as bass
from concourse import mybir

F32 = mybir.dt.float32
BF16 = mybir.dt.bfloat16
ALU = mybir.AluOpType
ACT = mybir.ActivationFunctionType
X = mybir.AxisListType.X

P = 128
B, C, H, W = 2, 256, 64, 64
PIX = H * W
CH = C // 2
KT = C // P
LK = CH * H
HALF = W
CHUNK = 512
ROWS = CHUNK // W
CHUNKS = PIX // CHUNK
GROUP = 512
QT = GROUP // P
GROUPS = LK // GROUP
UNITS = LK // (2 * P)
MAXCH = QT * LK // 512
KCH = LK // 512
TURNS = UNITS // 4 - 1
VX = 2 * W + 1

WS = 8
NH = 8
HD = C // NH
HP = NH // 2
HID = 1024
FT = HID // P
GK = 9
PADW = W + GK - 1
QC = P // 4
GE = (GK + 1) // 2
BANDS = 4
LINE = 128
EPS = 1e-5
SCALE = 4.0

VEC = {}
_n = 0
for _name, _w in (("b_g", 1), ("b_out", KT), ("norm1_g", KT), ("norm1_b", KT), ("qkv_b", 3 * KT), ("proj_b", KT),
                  ("gaze_b", KT), ("norm2_g", KT), ("norm2_b", KT), ("fc1_b", FT), ("fc2_b", KT)):
    VEC[_name] = _n
    _n += _w
NVEC = _n


def nonlocal_part(nc, x, wqk, bqk, wg, wout, vec, ident, x1):
    with ExitStack() as ctx:
        def sb(name, shape, dt=F32):
            return ctx.enter_context(nc.sbuf_tensor(name, shape, dt))

        def sem(name):
            return ctx.enter_context(nc.semaphore(name))

        wqk_sb = sb("wqk_sb", [P, KT, 2 * CH])
        bqk_sb = sb("bqk_sb", [P, 2 * CH])
        wg_sb = sb("wg_sb", [P, KT, CH])
        wout_sb = sb("wout_sb", [P, C])
        vec_sb = sb("vec_sb1", [P, NVEC])
        ident_sb = sb("ident_sb1", [P, P])
        x_ring = sb("x_ring", [P, 2, KT, ROWS, 2, W])
        proj = sb("proj", [P, 2, 2, 2 * CH])
        q1 = sb("q1", [P, LK], BF16)
        q2 = sb("q2", [P, LK], BF16)
        kh = sb("kh", [P, LK], BF16)
        kl = sb("kl", [P, LK], BF16)
        g_sb = sb("g_sb", [P, H, VX], BF16)
        probs = sb("probs", [P, 2, 2 * GROUP])
        p_high = sb("p_high", [P, 4, 2 * GROUP], BF16)
        p_low = sb("p_low", [P, 4, 2 * GROUP], BF16)
        chunk_max = sb("chunk_max", [P, KCH, QT])
        qmax = sb("qmax", [P, QT])
        neg_max = sb("neg_max", [P, QT])
        rden = sb("rden", [P, QT])
        o_high = sb("o_high", [P, QT * W])
        o_low = sb("o_low", [P, QT * W])
        o_grp = sb("o_grp", [P, QT * W])
        x_res = sb("x_res", [P, KT, QT * W])
        y = sb("y", [P, KT, QT * W])

        sT = ctx.enter_context(nc.psum_tensor("sT", [P, 2, 2, 512], F32))
        s_max = ctx.enter_context(nc.psum_tensor("s_max", [P, 2, 512], F32))
        acc = ctx.enter_context(nc.psum_tensor("acc", [P, 2, 512], F32))
        shift_ps, out_ps = s_max[:, 0], s_max[:, 1]

        weights_landed = sem("weights_landed")
        x_landed = [sem("x_landed0"), sem("x_landed1")]
        qk_projected = sem("qk_projected")
        qk_biased = sem("qk_biased")
        high_done = sem("high_done")
        split_done = sem("split_done")
        g_projected = sem("g_projected")
        g_high = sem("g_high")
        g_ready = sem("g_ready")
        kl_zeroed = sem("kl_zeroed")
        max_scored = sem("max_scored")
        max_free = sem("max_free")
        qmax_done = sem("qmax_done")
        neg_ready = sem("neg_ready")
        row_done = sem("row_done")
        row_high = sem("row_high")
        shift_ready = sem("shift_ready")
        scored = sem("scored")
        probs_ready = sem("probs_ready")
        high_ready = sem("high_ready")
        low_ready = sem("low_ready")
        low_ready2 = sem("low_ready2")
        pv_done = sem("pv_done")
        rden_done = sem("rden_done")
        normed = sem("normed")
        out_projected = sem("out_projected")
        res_landed = sem("res_landed")
        y_ready = sem("y_ready")
        y_stored = sem("y_stored")

        LOADS = 6
        block = ctx.enter_context(nc.Block())

        @block.sync
        def _(sp):
            for dst, src in ((wqk_sb[:], wqk.rearrange("(k p) o -> p k o", p=P)), (bqk_sb[:], bqk),
                             (wg_sb[:], wg.rearrange("(k p) o -> p k o", p=P)), (wout_sb[:], wout),
                             (vec_sb[:], vec), (ident_sb[:], ident)):
                sp.dma_start(dst, src).then_inc(weights_landed, 16)
            with sp.Fori(0, B) as b:
                with sp.Fori(0, CHUNKS // 2) as i:
                    for k in range(2):
                        sp.wait_ge(g_projected, b * CHUNKS + 2 * i + 1)
                        for kt in range(KT):
                            for copy in range(2):
                                sp.dma_start(x_ring[:, k, kt, :, copy], x[b, kt * P:(kt + 1) * P, bass.ts(
                                    2 * i + k, CHUNK)].rearrange("p (r w) -> p r w", w=W)).then_inc(x_landed[k], 16)
                with sp.Fori(0, GROUPS) as g:
                    sp.wait_ge(y_ready, b * GROUPS + g + 1)
                    sp.dma_start(x_res[:], x[b].rearrange("(k p) n -> p k n", p=P)[
                        :, :, bass.ts(g, QT * W)]).then_inc(res_landed, 16)
                    sp.wait_ge(y_ready, b * GROUPS + g + 2)
                    sp.dma_start(x1[b].rearrange("(k p) n -> p k n", p=P)[:, :, bass.ts(g, QT * W)],
                                 y[:]).then_inc(y_stored, 16)
            sp.wait_ge(y_stored, 16 * (B * GROUPS + 1))

        @block.tensor
        def _(pe):
            def score_max(n, t, kc, buf):
                pe.wait_ge(max_free, n + 1)
                nc.tensor.matmul(s_max[:, buf], q1[:, bass.ts(t, P)], kh[:, bass.ts(kc, 512)], start=True,
                                 stop=True).then_inc(max_scored, 1)

            def score_t(unit, g, u, buf, free):
                if free:
                    pe.wait_ge(high_ready, unit - 1)
                qs = bass.ts(g, GROUP)
                for k in range(2):
                    ks = bass.ts(2 * u + k, P)
                    nc.tensor.matmul(sT[:, buf, k], kh[:, ks], q1[:, qs], start=True, stop=False)
                    last = nc.tensor.matmul(sT[:, buf, k], kl[:, ks], q2[:, qs], start=False, stop=True)
                last.then_inc(scored, 1)

            def weigh(unit, u, buf, first=False):
                for k, low in enumerate((low_ready, low_ready2)):
                    pe.wait_ge(low, unit + 1)
                    for t in range(QT):
                        out = acc[:, t // 2, (t % 2) * VX:(t % 2 + 1) * VX]
                        cols = slice(k * GROUP + t * P, k * GROUP + (t + 1) * P)
                        nc.tensor.matmul(out, p_high[:, buf, cols], g_sb[:, 2 * u + k, :],
                                         start=first and k == 0 and t % 2 == 0, stop=False, skip_group_check=True)
                        last = nc.tensor.matmul(out[:, 0:W + 1], p_low[:, buf, cols], g_sb[:, 2 * u + k, 0:W + 1],
                                                start=False, stop=False, skip_group_check=True)
                last.then_inc(pv_done, 1)

            def shift_rows(grp):
                pe.wait_ge(neg_ready, grp + 2)
                for t in range(QT):
                    last = nc.tensor.matmul(shift_ps[:, t * P:(t + 1) * P], neg_max[:, t:t + 1].to_broadcast([P, P]),
                                            ident_sb[:], start=True, stop=True)
                last.then_inc(row_done, 1)

            def group(grp, g, ahead):
                n0 = (grp + 1) * MAXCH

                def look(c):
                    if ahead:
                        score_max(n0 + c, (g + 1) * QT + c % QT, c // QT, c % 2)

                pe.wait_ge(shift_ready, grp + 1)
                u0 = grp * UNITS
                score_t(u0, g, 0, 0, False)
                score_t(u0 + 1, g, 1, 1, False)
                pe.wait_ge(y_ready, grp + 1)
                for c in range(4):
                    look(c)
                score_t(u0 + 2, g, 2, 0, True)
                for c in range(4, 8):
                    look(c)
                pe.wait_ge(normed, grp + 1)
                weigh(u0, 0, 0, first=True)
                with pe.Fori(0, TURNS) as i:
                    for j in range(4):
                        u = 4 * i + 2 + j
                        score_t(u0 + u + 1, g, u + 1, (j + 1) % 2, True)
                        if ahead:
                            for c in (2 * j, 2 * j + 1):
                                score_max(n0 + 8 * i + 8 + c, (g + 1) * QT + c % QT, 2 * i + 2 + c // QT, c % 2)
                        weigh(u0 + u - 1, u - 1, (j + 1) % 4)
                score_t(u0 + UNITS - 1, g, UNITS - 1, 1, True)
                weigh(u0 + UNITS - 3, UNITS - 3, 1)
                if ahead:
                    shift_rows(grp + 1)
                weigh(u0 + UNITS - 2, UNITS - 2, 2)
                weigh(u0 + UNITS - 1, UNITS - 1, 3)
                pe.wait_ge(normed, grp + 2)
                for ct in range(KT):
                    last = nc.tensor.matmul(out_ps[:, ct * QT * W:(ct + 1) * QT * W], wout_sb[:, ct * P:(ct + 1) * P],
                                            o_grp[:], start=True, stop=True)
                last.then_inc(out_projected, 1)

            pe.wait_ge(weights_landed, 16 * LOADS)
            with pe.Fori(0, B) as b:
                with pe.Fori(0, CHUNKS // 2) as i:
                    for k in range(2):
                        chunk = b * CHUNKS + 2 * i + k
                        pe.wait_ge(x_landed[k], 64 * (b * (CHUNKS // 2) + i) + 64)
                        for hh in range(ROWS // 2):
                            if hh >= 2:
                                pe.wait_ge(qk_biased, chunk * 4 + hh)
                            else:
                                pe.wait_ge(qk_biased, chunk * 4 + 1)
                            for j in range(2):
                                row = 2 * hh + j
                                for kt in range(KT):
                                    xs = x_ring[:, k, kt, row].rearrange("p c w -> p (c w)")
                                    last = nc.tensor.matmul(sT[:, hh % 2, 0, j * 2 * CH:(j + 1) * 2 * CH], xs,
                                                            wqk_sb[:, kt], start=kt == 0, stop=kt == KT - 1)
                            last.then_inc(qk_projected, 1)
                        pe.wait_ge(g_ready, chunk + 1)
                        for kt in range(KT):
                            last = nc.tensor.matmul(s_max[:, 0], wg_sb[:, kt], x_ring[:, k, kt, :, 0], start=kt == 0,
                                                    stop=kt == KT - 1)
                        last.then_inc(g_projected, 1)
                with pe.Fori(0, MAXCH // 8) as i:
                    pe.wait_ge(split_done, (b + 1) * CHUNKS * 4 + 1)
                    pe.wait_ge(g_ready, (b + 1) * CHUNKS + 1)
                    pe.wait_ge(y_ready, b * GROUPS + 1)
                    for c in range(8):
                        score_max(b * GROUPS * MAXCH + 8 * i + c, c % QT, 2 * i + c // QT, c % 2)
                shift_rows(b * GROUPS)
                with pe.Fori(0, GROUPS - 1) as g:
                    group(b * GROUPS + g, g, True)
                group(b * GROUPS + GROUPS - 1, GROUPS - 1, False)

        @block.scalar
        def _(act):
            act.wait_ge(weights_landed, 16 * LOADS)

            def exponent(unit, buf, reused, reused_high):
                act.wait_ge(scored, unit + 1)
                if reused:
                    act.wait_ge(low_ready, unit - 1)
                    act.wait_ge(low_ready2, unit - 1)
                src = sT[:, buf % 2].rearrange("p k n -> p (k n)")
                nc.scalar.activation(probs[:, buf % 2], src, ACT.Exp).then_inc(probs_ready, 1)
                if reused_high:
                    act.wait_ge(pv_done, unit - 3)
                nc.scalar.activation(p_high[:, buf], src, ACT.Exp).then_inc(high_ready, 1)

            with act.Fori(0, B) as b:
                with act.Fori(0, CHUNKS) as c:
                    chunk = b * CHUNKS + c
                    for hh in range(ROWS // 2):
                        act.wait_ge(qk_biased, chunk * 4 + hh + 2)
                        pr = proj[:, hh % 2]
                        cols = bass.ds(c * ROWS * CH + hh * 2 * CH, 2 * CH)

                        def two(t, lo=0, hi=P):
                            return t[lo:hi, cols].rearrange("p (r o) -> p r o", r=2)
                        nc.scalar.copy(two(q1), pr[:, :, 0:CH])
                        nc.scalar.copy(two(kh), pr[:, :, CH:2 * CH])
                        nc.scalar.copy(two(q2, 0, HALF), pr[0:HALF, :, 0:CH]).then_inc(high_done, 1)
                    act.wait_ge(g_projected, chunk + 2)
                    nc.scalar.activation(g_sb[:, bass.ts(c, ROWS), 0:W], s_max[:, 0].rearrange("p (r w) -> p r w", w=W),
                                         ACT.Identity, bias=vec_sb[:, VEC["b_g"]:VEC["b_g"] + 1]).then_inc(g_high, 1)
                with act.Fori(0, GROUPS) as g:
                    u0 = (b * GROUPS + g) * UNITS
                    for u in range(4):
                        exponent(u0 + u, u, u >= 2, False)
                    with act.Fori(0, TURNS) as i:
                        for k in range(4):
                            exponent(u0 + 4 * i + 4 + k, k, True, True)

        @block.gpsimd
        def _(pool):
            for s in (qk_biased, split_done, g_ready, g_projected, normed, neg_ready, y_ready):
                pool.sem_inc(s, 1)
            pool.sem_inc(y_stored, 16)
            with pool.Fori(0, B * GROUPS * UNITS // 4) as i:
                for buf in range(4):
                    pool.wait_ge(high_ready, 4 * i + buf + 1)
                    nc.gpsimd.tensor_tensor(p_low[:, buf, GROUP:], probs[:, buf % 2, GROUP:], p_high[:, buf, GROUP:],
                                            ALU.subtract).then_inc(low_ready2, 1)

        @block.vector
        def _(dve):
            def maximum(n0, c, buf):
                dve.wait_ge(max_scored, n0 + c + 1)
                nc.vector.tensor_reduce(chunk_max_flat[:, bass.ds(c, 1)], s_max[:, buf], X,
                                        ALU.max).then_inc(max_free, 1)

            def low_probs(unit, buf):
                dve.wait_ge(high_ready, unit + 1)
                nc.vector.tensor_tensor(p_low[:, buf, 0:GROUP], probs[:, buf % 2, 0:GROUP], p_high[:, buf, 0:GROUP],
                                        ALU.subtract).then_inc(low_ready, 1)

            def negate(grp):
                dve.wait_ge(max_free, 2 + (grp + 1) * MAXCH)
                dve.wait_ge(neg_ready, grp + 1)
                nc.vector.tensor_reduce(qmax[:], chunk_max[:].rearrange("p k t -> p t k"), X, ALU.max).then_inc(qmax_done, 1)
                dve.wait_ge(qmax_done, grp + 1)
                nc.vector.tensor_scalar(neg_max[:], qmax[:], -1.0, None, ALU.mult).then_inc(neg_ready, 1)

            def write_shift(grp, g):
                cols = bass.ts(g, GROUP)
                dve.wait_ge(row_done, grp + 1)
                nc.vector.tensor_copy(q2[HALF:P, cols], shift_ps[HALF:P, :]).then_inc(row_high, 1)
                dve.wait_ge(row_high, grp + 1)
                nc.vector.tensor_tensor(q2[HALF + 32:P, cols], shift_ps[HALF + 32:P, :], q2[HALF + 32:P, cols],
                                        ALU.subtract).then_inc(shift_ready, 1)

            def group(grp, g, ahead):
                n0 = (grp + 1) * MAXCH
                u0 = grp * UNITS

                def look(c, buf):
                    if ahead:
                        maximum(n0, c, buf)
                for c in range(4):
                    look(c, c % 2)
                low_probs(u0, 0)
                for c in range(4, 8):
                    look(c, c % 2)
                with dve.Fori(0, TURNS) as i:
                    for j in range(4):
                        low_probs(u0 + 4 * i + 1 + j, (j + 1) % 4)
                        for c in (2 * j, 2 * j + 1):
                            look(8 * i + 8 + c, c % 2)
                low_probs(u0 + UNITS - 3, 1)
                if ahead:
                    negate(grp + 1)
                low_probs(u0 + UNITS - 2, 2)
                if ahead:
                    write_shift(grp + 1, g + 1)
                low_probs(u0 + UNITS - 1, 3)
                dve.wait_ge(pv_done, (grp + 1) * UNITS)
                outs = acc[:, :, 0:2 * VX].rearrange("p b (t w) -> p b t w", t=2)

                def tiles(a):
                    return a.rearrange("p (b t w) -> p b t w", b=2, t=2)
                for bank in range(2):
                    last = nc.vector.reciprocal(rden[:, 2 * bank:2 * bank + 2].unsqueeze(2), outs[:, bank, :, W:W + 1])
                last.then_inc(rden_done, 1)
                dve.wait_ge(rden_done, 3 * grp + 1)
                scale = tiles(rden[:]).to_broadcast([P, 2, 2, W])
                nc.vector.tensor_tensor(tiles(o_low[:]), outs[:, :, :, W + 1:VX], scale, ALU.mult).then_inc(rden_done, 1)
                nc.vector.tensor_tensor(tiles(o_high[:]), outs[:, :, :, 0:W], scale, ALU.mult).then_inc(rden_done, 1)
                dve.wait_ge(rden_done, 3 * grp + 3)
                nc.vector.tensor_tensor(o_grp[:], o_high[:], o_low[:], ALU.add).then_inc(normed, 1)
                dve.wait_ge(out_projected, grp + 1)
                dve.wait_ge(res_landed, 16 * (grp + 1))
                dve.wait_ge(y_stored, 16 * grp + 16)
                for ct in range(KT):
                    last = nc.vector.scalar_tensor_tensor(
                        y[:, ct], out_ps[:, ct * QT * W:(ct + 1) * QT * W],
                        vec_sb[:, VEC["b_out"] + ct:VEC["b_out"] + ct + 1], x_res[:, ct], ALU.add, ALU.add)
                last.then_inc(y_ready, 1)

            chunk_max_flat = chunk_max[:].rearrange("p k t -> p (k t)")
            dve.wait_ge(weights_landed, 16 * LOADS)
            nc.vector.memset(chunk_max[:, 0], 0.0).then_inc(max_free, 1)
            nc.vector.memset(chunk_max[:, 1], 0.0).then_inc(max_free, 1)
            nc.vector.memset(g_sb[:, :, W:W + 1], 1.0)
            nc.vector.memset(kl[HALF:P, :].bitcast(F32), 0.0).then_inc(kl_zeroed, 1)
            dve.wait_ge(kl_zeroed, 1)
            nc.vector.memset(kl[HALF:HALF + 1, :], 1.0)
            nc.vector.memset(kl[HALF + 32:HALF + 33, :], 1.0)
            with dve.Fori(0, B) as b:
                nc.vector.memset(q2[HALF:P, :].bitcast(F32), 0.0)
                with dve.Fori(0, CHUNKS) as c:
                    chunk = b * CHUNKS + c

                    def bias(hh):
                        dve.wait_ge(split_done, chunk * 4 + (hh if hh >= 2 else 1))
                        dve.wait_ge(qk_projected, chunk * 4 + hh + 1)
                        nc.vector.tensor_tensor(proj[:, hh % 2], sT[:, hh % 2, 0].rearrange("p (r o) -> p r o", r=2),
                                                bqk_sb[:].unsqueeze(1).to_broadcast([P, 2, 2 * CH]),
                                                ALU.add).then_inc(qk_biased, 1)

                    def low(hh):
                        dve.wait_ge(high_done, chunk * 4 + hh + 1)
                        cols = bass.ds(c * ROWS * CH + hh * 2 * CH, 2 * CH)
                        pr = proj[:, hh % 2]
                        ql = q1[HALF:P, cols].rearrange("p (r o) -> p r o", r=2)
                        nc.vector.tensor_tensor(ql, pr[HALF:P, :, 0:CH], ql, ALU.subtract)
                        nc.vector.tensor_tensor(kl[0:HALF, cols].rearrange("p (r o) -> p r o", r=2),
                                                pr[0:HALF, :, CH:2 * CH],
                                                kh[0:HALF, cols].rearrange("p (r o) -> p r o", r=2),
                                                ALU.subtract).then_inc(split_done, 1)
                    bias(0)
                    bias(1)
                    low(0)
                    bias(2)
                    low(1)
                    bias(3)
                    low(2)
                    low(3)
                    dve.wait_ge(g_high, chunk + 1)
                    rows = g_sb[:, bass.ts(c, ROWS)]
                    nc.vector.scalar_tensor_tensor(rows[:, :, W + 1:VX], s_max[:, 0].rearrange("p (r w) -> p r w", w=W),
                                                   vec_sb[:, VEC["b_g"]:VEC["b_g"] + 1], rows[:, :, 0:W],
                                                   ALU.add, ALU.subtract).then_inc(g_ready, 1)
                with dve.Fori(0, MAXCH // 2) as i:
                    for k in range(2):
                        maximum(b * GROUPS * MAXCH, 2 * i + k, k)
                negate(b * GROUPS)
                write_shift(b * GROUPS, 0)
                with dve.Fori(0, GROUPS - 1) as g:
                    group(b * GROUPS + g, g, True)
                group(b * GROUPS + GROUPS - 1, GROUPS - 1, False)


def window_part(nc, x1, qkvw, bv, rpb, vec, ident, v_img, o_att):
    with ExitStack() as ctx:
        def sb(name, shape, dt=F32):
            return ctx.enter_context(nc.sbuf_tensor("window_" + name, shape, dt))

        def sem(name):
            return ctx.enter_context(nc.semaphore("window_" + name))

        qkvw_sb = sb("qkvw_sb", [P, KT, 3 * C])
        bv_sb = sb("bv_sb", [P, C])
        rpb_sb = sb("rpb_sb", [P, HP * WS * WS])
        vec_sb = sb("vec_sb2", [P, NVEC])
        ident_sb = sb("ident_sb2", [P, P])
        mean_w = sb("mean_w", [P, P])
        eps = sb("eps", [P, 1])
        x_in = sb("x_in", [P, 2, KT, CHUNK])
        xc = sb("xc", [P, KT, CHUNK])
        sq = sb("sq", [P, KT, CHUNK])
        std = sb("std", [P, CHUNK])
        rstd = sb("rstd", [P, CHUNK])
        xh = sb("xh", [P, KT, CHUNK])
        xn = sb("xn", [P, KT, CHUNK])
        qm = sb("qm", [P, KT, 2, W // WS, 2, WS * WS])
        qb4 = sb("qb4", [P, KT])
        k_sb = sb("k_sb", [P, KT, CHUNK])
        vt = sb("vt", [P, 2, 4, C])
        att = sb("att", [P, 2, CHUNK])
        amax = sb("amax", [P, 2, NH])
        den = sb("den", [P, 2, NH])
        rden = sb("rden2", [P, 2, NH])
        attT = sb("attT", [P, 2, CHUNK])
        o_sb = sb("o_sb", [P, 2, KT, CHUNK])

        def bank(name):
            return ctx.enter_context(nc.psum_tensor("window_" + name, [P, 512], F32))

        pj = [bank("pj0"), bank("pj1")]
        sc = [bank("sc0"), bank("sc1")]
        tp = [bank("tp0"), bank("tp1")]
        ob = [bank("ob0"), bank("ob1")]

        weights_landed = sem("weights_landed2")
        setup_done = sem("setup_done")
        x_landed = [sem("xin_landed0"), sem("xin_landed1")]
        mean_done = sem("mean_done")
        centered = sem("centered")
        squared = sem("squared")
        var_done = sem("var_done")
        std_done = sem("std_done")
        rstd_done = sem("rstd_done")
        scaled = sem("scaled")
        xn_ready = sem("xn_ready")
        projected = sem("projected")
        q_ready = [sem("q_ready0"), sem("q_ready1")]
        k_ready = [sem("k_ready0"), sem("k_ready1")]
        vt_ready = sem("vt_ready")
        att_scored = sem("att_scored")
        att_biased = sem("att_biased")
        amax_done = sem("amax_done")
        shifted = sem("shifted")
        exped = sem("exped")
        den_done = sem("den_done")
        rden_done = sem("rden_done2")
        att_ready = sem("att_ready")
        transposed = sem("transposed")
        attT_ready = sem("attT_ready")
        weighing = sem("weighing")
        attended = sem("attended")
        o_copied = sem("o_copied")
        v_stored = [sem("v_stored0"), sem("v_stored1")]
        o_stored = [sem("o_stored0"), sem("o_stored1")]

        LOADS = 5
        PAIRS = 4
        SLOTS = 6

        def v(name, kt=0):
            return vec_sb[:, VEC[name] + kt:VEC[name] + kt + 1]

        def win(t):
            return t.rearrange("p (c r s) -> p r c s", c=W // WS, r=WS)

        def v_col(h):
            return (2 * (h % 4) + h // 4) * HD

        def qm_head(rows, kt, r):
            return qm[rows, kt, r // 2, :, r % 2, :]

        block = ctx.enter_context(nc.Block())

        @block.sync
        def _(sp):
            for dst, src in ((qkvw_sb[:], qkvw.rearrange("(k p) o -> p k o", p=P)), (bv_sb[:], bv), (rpb_sb[:], rpb),
                             (vec_sb[:], vec), (ident_sb[:], ident)):
                sp.dma_start(dst, src).then_inc(weights_landed, 16)

            def load(b, i, k):
                sp.dma_start(x_in[:, k], x1[b].rearrange("(k p) n -> p k n", p=P)[
                    :, :, bass.ts(i, CHUNK)]).then_inc(x_landed[k], 16)

            with sp.Fori(0, B) as b:
                with sp.Fori(0, CHUNKS // 2) as i:
                    for k in range(2):
                        it = b * CHUNKS + 2 * i + k
                        sp.wait_ge(centered, it + 1)
                        load(b, 2 * i + k, k)
                        sp.wait_ge(vt_ready, it * 2 + 4)
                        rows = v_img[b].rearrange("q (r i) (s c) n -> i c r s q n", i=WS, c=WS)[bass.ds(2 * i + k, 1)]
                        for c in range(W // WS):
                            half = slice(64 * (c % 2), 64 * (c % 2) + 64)
                            for q in range(4):
                                sp.dma_start(rows[0, c, :, :, q], vt[half, k, c // 2, 64 * q:64 * q + 64]).then_inc(
                                    v_stored[k], 16)
            for k in range(2):
                sp.wait_ge(v_stored[k], 16 * 32 * (B * CHUNKS // 2) + 1)
                sp.wait_ge(o_stored[k], 16 * (B * CHUNKS // 2) + 1)

        @block.gpsimd
        def _(pool):
            for s in (centered, scaled, xn_ready, vt_ready, vt_ready, o_copied, att_biased, att_biased, transposed,
                      transposed, attT_ready, attT_ready, attended, attended, *v_stored, *o_stored):
                pool.sem_inc(s, 1)
            with pool.Fori(0, B * CHUNKS) as it:
                def subtract(p):
                    pool.wait_ge(amax_done, it * PAIRS + p + 1)
                    a = att[:, p % 2].rearrange("p (g m) -> p g m", g=NH)
                    nc.gpsimd.tensor_tensor(a, a, amax[:, p % 2].unsqueeze(2).to_broadcast([P, NH, WS * WS]),
                                            ALU.subtract).then_inc(shifted, 1)

                def normalise(p):
                    pool.wait_ge(rden_done, it * PAIRS + p + 1)
                    a = att[:, p % 2].rearrange("p (g m) -> p g m", g=NH)
                    nc.gpsimd.tensor_tensor(a, a, rden[:, p % 2].unsqueeze(2).to_broadcast([P, NH, WS * WS]),
                                            ALU.mult).then_inc(att_ready, 1)
                subtract(0)
                for p in range(1, PAIRS):
                    subtract(p)
                    normalise(p - 1)
                normalise(PAIRS - 1)

        @block.tensor
        def _(pe):
            def norm(n, src, landed):
                landed()
                pe.wait_ge(centered, n + 1)
                for kt in range(KT):
                    last = nc.tensor.matmul(pj[0][:], mean_w[:], src(kt), start=kt == 0, stop=kt == KT - 1)
                last.then_inc(mean_done, 1)
                pe.wait_ge(squared, n + 1)
                for kt in range(KT):
                    last = nc.tensor.matmul(pj[1][:], mean_w[:], sq[:, kt], start=kt == 0, stop=kt == KT - 1)
                last.then_inc(var_done, 1)

            def qkv(it, n):
                def project(bank, col):
                    for kt in range(KT):
                        last = nc.tensor.matmul(bank[:], qkvw_sb[:, kt, col:col + P], xn[:, kt],
                                                start=kt == 0, stop=kt == KT - 1)
                    last.then_inc(projected, 1)
                pe.wait_ge(xn_ready, n + 2)
                for ct in range(KT):
                    project(pj[ct], ct * P)
                for ct in range(KT):
                    pe.wait_ge(q_ready[ct], it + 1)
                    project(pj[ct], C + ct * P)
                for h in range(2):
                    pe.wait_ge(k_ready[h], it + 1)
                    for p in range(2):
                        t = (2 * h + p) * P
                        for kt in range(KT):
                            last = nc.tensor.matmul(pj[h][:, p * C:(p + 1) * C], xn[:, kt, t:t + P],
                                                    qkvw_sb[:, kt, 2 * C:3 * C], start=kt == 0, stop=kt == KT - 1)
                    last.then_inc(projected, 1)

            def scores(wp, p):
                pe.wait_ge(att_biased, wp + 1)
                for w in range(2):
                    t = p * P + w * WS * WS
                    for hp in range(HP):
                        lhsT = qm[:, hp // 2, hp % 2, 2 * p + w].rearrange("p b t -> p (b t)")
                        last = nc.tensor.matmul(sc[p % 2][:, (2 * hp + w) * 64:(2 * hp + w + 1) * 64], lhsT,
                                                k_sb[:, hp // 2, t:t + WS * WS], start=True, stop=True)
                last.then_inc(att_scored, 1)

            def turn(wp, p):
                pe.wait_ge(att_ready, wp + 1)
                pe.wait_ge(attT_ready, wp + 1)
                for hp in range(HP):
                    last = nc.tensor.transpose(tp[p % 2][:, hp * P:(hp + 1) * P], att[:, p % 2, hp * P:(hp + 1) * P], ident_sb[:])
                last.then_inc(transposed, 1)

            def weigh(it, wp, p, k):
                pe.wait_ge(attT_ready, wp + 3)
                if p == 0:
                    pe.wait_ge(o_copied, it + 1)
                pe.sem_inc(weighing, 1)
                for w in range(2):
                    for h in range(NH):
                        r = h % 4
                        col = (p * KT + h // 4) * 64
                        last = nc.tensor.matmul(ob[w][32 * r:32 * r + 32, col:col + 64],
                                                vt[64 * w:64 * w + 64, k, p, v_col(h):v_col(h) + HD],
                                                attT[64 * w:64 * w + 64, p % 2, h * 64:(h + 1) * 64],
                                                start=True, stop=True)
                last.then_inc(attended, 1)

            pe.wait_ge(weights_landed, 16 * LOADS)
            pe.wait_ge(setup_done, 3)
            with pe.Fori(0, B) as b:
                with pe.Fori(0, CHUNKS // 2) as i:
                    for k in range(2):
                        it = b * CHUNKS + 2 * i + k
                        n = it

                        def landed():
                            pe.wait_ge(x_landed[k], 16 * (b * CHUNKS // 2 + i + 1))
                            pe.wait_ge(vt_ready, it * 2 + 2)
                        norm(n, lambda kt: x_in[:, k, kt], landed)
                        qkv(it, n)
                        pe.wait_ge(q_ready[1], it + 1)
                        pe.wait_ge(k_ready[1], it + 1)
                        pe.wait_ge(k_ready[0], it + 1)
                        wp = it * PAIRS
                        scores(wp, 0)
                        scores(wp + 1, 1)
                        pe.wait_ge(vt_ready, it * 2 + 4)
                        for p in range(PAIRS):
                            if p + 2 < PAIRS:
                                scores(wp + p + 2, p + 2)
                            turn(wp + p, p)
                            if p:
                                weigh(it, wp + p - 1, p - 1, k)
                        weigh(it, wp + PAIRS - 1, PAIRS - 1, k)

        @block.scalar
        def _(act):
            act.wait_ge(weights_landed, 16 * LOADS)
            act.wait_ge(setup_done, 3)

            def norm(n, dst):
                act.wait_ge(centered, n + 2)
                nc.scalar.activation(sq[:], xc[:], ACT.Square).then_inc(squared, 1)
                act.wait_ge(var_done, n + 1)
                nc.scalar.activation(std[:], pj[1][:], ACT.Sqrt, bias=eps[:]).then_inc(std_done, 1)
                act.wait_ge(scaled, n + 2)
                dst()

            def affine(g, bias, order):
                for kt in range(KT):
                    src = xh[:, kt]
                    dst = xn[:, kt]
                    if order:
                        src, dst = src.rearrange("p (r c s) -> p r c s", r=WS, s=WS), win(dst)
                    last = nc.scalar.activation(dst, src, ACT.Identity, scale=v(g, kt), bias=v(bias, kt))
                last.then_inc(xn_ready, 1)

            with act.Fori(0, B) as b, act.Fori(0, CHUNKS // 2) as i:
                for k in range(2):
                    it = b * CHUNKS + 2 * i + k
                    n = it
                    norm(n, lambda: affine("norm1_g", "norm1_b", True))
                    act.wait_ge(projected, it * SLOTS + 1)
                    for r in range(4):
                        rows = slice(32 * r, 32 * r + 32)
                        last = nc.scalar.activation(qm_head(rows, 0, r), pj[0][rows, :].rearrange(
                            "p (c t) -> p c t", c=WS), ACT.Identity, scale=SCALE, bias=qb4[rows, 0:1])
                    last.then_inc(q_ready[0], 1)
                    act.wait_ge(projected, it * SLOTS + 3)
                    nc.scalar.activation(k_sb[:, 0], pj[0][:], ACT.Identity, bias=v("qkv_b", 2)).then_inc(k_ready[0], 1)

                    def exponent(p):
                        act.wait_ge(shifted, it * PAIRS + p + 1)
                        nc.scalar.activation(att[:, p % 2], att[:, p % 2], ACT.Exp).then_inc(exped, 1)

                    def copy_turned(p):
                        act.wait_ge(transposed, it * PAIRS + p + 3)
                        act.wait_ge(attended, it * PAIRS + p + 1)
                        nc.scalar.copy(attT[:, p % 2], tp[p % 2][:]).then_inc(attT_ready, 1)
                    exponent(0)
                    exponent(1)
                    for p in range(PAIRS):
                        copy_turned(p)
                        if p + 2 < PAIRS:
                            exponent(p + 2)
                    act.wait_ge(attended, (it + 1) * PAIRS + 2)
                    act.wait_ge(o_stored[k], 16 * (b * CHUNKS // 2 + i) + 1)
                    for w in range(2):
                        for kt in range(KT):
                            src = ob[w][:].rearrange("p (q k r s) -> p k q r s", k=KT, r=WS, s=WS)[:, kt]
                            dst = o_sb[:, k, kt].rearrange("p (r s q w) -> p w q r s", r=WS, s=WS, w=2)[:, w]
                            last = nc.scalar.activation(dst, src, ACT.Identity, bias=v("gaze_b", kt))
                    last.then_inc(o_copied, 1)
                    act.wait_ge(o_copied, it + 2)
                    act.dma_start(o_att[b, bass.ds(2 * i + k, 1)].rearrange("a (k p) n -> p (a k) n", p=P),
                                  o_sb[:, k]).then_inc(o_stored[k], 16)

        @block.vector
        def _(dve):
            nc.vector.memset(mean_w[:], 1.0 / C)
            nc.vector.memset(eps[:], EPS).then_inc(setup_done, 1)
            nc.vector.memset(qm[:], 0.0).then_inc(setup_done, 1)
            dve.wait_ge(weights_landed, 16 * LOADS)
            nc.vector.tensor_scalar(qb4[:], vec_sb[:, VEC["qkv_b"]:VEC["qkv_b"] + KT], SCALE, None,
                                    ALU.mult).then_inc(setup_done, 1)
            dve.wait_ge(setup_done, 3)

            def norm(n, src):
                dve.wait_ge(mean_done, n + 1)
                dve.wait_ge(scaled, n + 1)
                for kt in range(KT):
                    last = nc.vector.tensor_tensor(xc[:, kt], src(kt), pj[0][:], ALU.subtract)
                last.then_inc(centered, 1)
                dve.wait_ge(std_done, n + 1)
                nc.vector.reciprocal(rstd[:], std[:]).then_inc(rstd_done, 1)
                dve.wait_ge(rstd_done, n + 1)
                dve.wait_ge(xn_ready, n + 1)
                for kt in range(KT):
                    last = nc.vector.tensor_tensor(xh[:, kt], xc[:, kt], rstd[:], ALU.mult)
                last.then_inc(scaled, 1)

            with dve.Fori(0, B) as b:
                with dve.Fori(0, CHUNKS // 2) as i:
                    for k in range(2):
                        it = b * CHUNKS + 2 * i + k
                        norm(it, lambda kt: x_in[:, k, kt])
                        dve.wait_ge(projected, it * SLOTS + 2)
                        for r in range(4):
                            rows = slice(32 * r, 32 * r + 32)
                            last = nc.vector.tensor_scalar(qm_head(rows, 1, r), pj[1][rows, :].rearrange(
                                "p (c t) -> p c t", c=WS), SCALE, qb4[rows, 1:2], ALU.mult, ALU.add)
                        last.then_inc(q_ready[1], 1)
                        dve.wait_ge(projected, it * SLOTS + 4)
                        nc.vector.tensor_scalar(k_sb[:, 1], pj[1][:], v("qkv_b", 3), None, ALU.add).then_inc(k_ready[1], 1)
                        dve.wait_ge(v_stored[k], 16 * 32 * (b * CHUNKS // 2 + i) + 1)
                        for h in range(2):
                            dve.wait_ge(projected, it * SLOTS + 5 + h)
                            nc.vector.tensor_tensor(vt[:, k, 2 * h:2 * h + 2],
                                                    pj[h][:].rearrange("p (q c) -> p q c", q=2),
                                                    bv_sb[:].unsqueeze(1).to_broadcast([P, 2, C]),
                                                    ALU.add).then_inc(vt_ready, 1)

                        def bias_and_max(p):
                            wp = it * PAIRS + p
                            dve.wait_ge(att_scored, wp + 1)
                            dve.wait_ge(transposed, wp + 1)
                            def by_window(a):
                                return a.rearrange("p (h w m) -> p h w m", h=HP, w=2)
                            nc.vector.tensor_tensor(by_window(att[:, p % 2]), by_window(sc[p % 2][:]),
                                                    rpb_sb[:].rearrange("p (h m) -> p h m", h=HP).unsqueeze(2)
                                                    .to_broadcast([P, HP, 2, WS * WS]),
                                                    ALU.add).then_inc(att_biased, 1)
                            dve.wait_ge(att_biased, wp + 3)
                            nc.vector.tensor_reduce(amax[:, p % 2], att[:, p % 2].rearrange("p (g m) -> p g m", g=NH),
                                                    X, ALU.max).then_inc(amax_done, 1)

                        def denominators(p):
                            wp = it * PAIRS + p
                            dve.wait_ge(exped, wp + 1)
                            nc.vector.tensor_reduce(den[:, p % 2], att[:, p % 2].rearrange("p (g m) -> p g m", g=NH),
                                                    X, ALU.add).then_inc(den_done, 1)
                            dve.wait_ge(den_done, wp + 1)
                            nc.vector.reciprocal(rden[:, p % 2], den[:, p % 2]).then_inc(rden_done, 1)
                        bias_and_max(0)
                        bias_and_max(1)
                        for p in range(PAIRS):
                            denominators(p)
                            if p + 2 < PAIRS:
                                bias_and_max(p + 2)


def conv_part(nc, v_img, taps, gz):
    with ExitStack() as ctx:
        def sb(name, shape, dt=F32):
            return ctx.enter_context(nc.sbuf_tensor("conv_" + name, shape, dt))

        def sem(name):
            return ctx.enter_context(nc.semaphore("conv_" + name))

        v_sb = sb("v_sb", [P, 2, B, PADW, 2 * QC])
        band = sb("band", [P, BANDS, KT, 4, GE, H])
        v_ch = sb("v_ch", [P, 2, KT, 4, B, PADW])
        conv = [ctx.enter_context(nc.psum_tensor(f"conv{k}", [P, 4, B * W], F32)) for k in range(2)]

        padding_done = sem("padding_done")
        v_landed = [sem("v_landed0"), sem("v_landed1")]
        band_landed = [sem(f"band_landed{k}") for k in range(BANDS)]
        v_split = sem("v_split")
        convolving = sem("convolving")
        convolved = sem("convolved")
        gz_copied = sem("gz_copied")

        PERQ = QC // 4
        GROUPS8 = 4 * PERQ

        block = ctx.enter_context(nc.Block())

        @block.sync
        def _(sp):
            with sp.Fori(0, GROUPS8 // BANDS) as t:
                for s in range(BANDS):
                    sp.wait_ge(convolved, t * BANDS + s + 1)
                    for kt in range(KT):
                        for half in range(2):
                            line = taps[bass.ds(kt * P + (t * BANDS + s) * 4, 1), half, 0:1]
                            src = bass.AP(tensor=line.tensor, offset=line.offset,
                                          ap=[[1, H], [2 * LINE, 4 * GE], [1, H]])
                            sp.dma_start(band[64 * half:64 * half + 64, s, kt].rearrange("p c e h -> p (c e) h"),
                                         src).then_inc(band_landed[s], 16)

        @block.gpsimd
        def _(pool):
            for s, n in ((convolved, BANDS), (gz_copied, 2)):
                pool.sem_inc(s, n)
            for k in range(2):
                nc.gpsimd.memset(v_sb[:, k], 0.0).then_inc(padding_done, 1)

        @block.scalar
        def _(act):
            def load(q):
                for b in range(B):
                    for half in range(2):
                        at = GK // 2 - half
                        act.dma_start(v_sb[64 * half:64 * half + 64, q % 2, b, at:at + W],
                                      v_img[b, q]).then_inc(v_landed[q % 2], 16)
            act.wait_ge(padding_done, 2)
            load(0)
            load(1)
            for q in range(4):
                act.wait_ge(v_landed[q % 2], 64 * (q // 2 + 1))
                with act.Fori(0, PERQ // 2) as j:
                    for s in range(2):
                        act.wait_ge(convolved, q * PERQ + 2 * j + s + BANDS - 1)
                        for kt in range(KT):
                            src = v_sb[:, q % 2, :, :, kt * QC:(kt + 1) * QC].rearrange("p b w c -> p c (b w)")
                            last = nc.scalar.activation(v_ch[:, s, kt].rearrange("p c b w -> p c (b w)"),
                                                        src[:, bass.ds(8 * j + 4 * s, 4)], ACT.Identity)
                        last.then_inc(v_split, 1)
                if q + 2 < 4:
                    act.wait_ge(v_split, (q + 1) * PERQ)
                    load(q + 2)

        @block.tensor
        def _(pe):
            with pe.Fori(0, GROUPS8 // BANDS) as t:
                for s in range(BANDS):
                    n = t * BANDS + s
                    pe.wait_ge(band_landed[s], 64 * t + 64)
                    pe.wait_ge(v_split, n + 1)
                    pe.wait_ge(gz_copied, n + 1)
                    pe.sem_inc(convolving, 1)
                    for c in range(4):
                        for kt in range(KT):
                            for e in range(GE):
                                last = nc.tensor.matmul(conv[s % 2][64 * kt:64 * kt + 64, c],
                                                        band[:, s, kt, c, e], v_ch[:, s % 2, kt, c, :, 2 * e:2 * e + W],
                                                        start=e == 0, stop=e == GE - 1)
                    last.then_inc(convolved, 1)

        @block.vector
        def _(dve):
            with dve.Fori(0, GROUPS8 // 2) as j:
                for s in range(2):
                    dve.wait_ge(convolved, 2 * j + s + 1 + BANDS)
                    nc.vector.tensor_copy(gz[:, bass.ds(8 * j + 4 * s, 4)], conv[s][:]).then_inc(gz_copied, 1)


def turn_part(nc, gz, o_att, flip, osum):
    with ExitStack() as ctx:
        flip_sb = ctx.enter_context(nc.sbuf_tensor("flip_sb", [P, P], F32))
        turned = [ctx.enter_context(nc.psum_tensor(f"turned{k}", [P, 4, KT, H], F32)) for k in range(4)]
        flip_landed = ctx.enter_context(nc.semaphore("flip_landed"))
        o_landed = ctx.enter_context(nc.semaphore("o_landed"))
        turned_done = ctx.enter_context(nc.semaphore("turned_done"))
        added = ctx.enter_context(nc.semaphore("added"))
        N = B * W // 4

        block = ctx.enter_context(nc.Block())

        @block.sync
        def _(sp):
            sp.dma_start(flip_sb[:], flip).then_inc(flip_landed, 16)
            for b in range(B):
                for kt in range(KT):
                    sp.dma_start(osum[:, kt, b * PIX:(b + 1) * PIX].rearrange("p (i n) -> p i n", i=CHUNKS),
                                 o_att[b, :, kt * P:(kt + 1) * P].rearrange("i p n -> p i n")).then_inc(o_landed, 16)

        @block.tensor
        def _(pe):
            pe.wait_ge(flip_landed, 16)
            for n in range(N):
                if n >= 4:
                    pe.wait_ge(added, n - 3)
                for j in range(4):
                    last = nc.tensor.matmul(turned[n % 4][:, j].rearrange("p k h -> p (k h)"), gz[:, :, 4 * n + j],
                                            flip_sb[:], start=True, stop=True)
                last.then_inc(turned_done, 1)

        @block.vector
        def _(dve):
            dve.wait_ge(o_landed, 16 * B * KT)
            for n in range(N):
                b, w = divmod(4 * n, W)
                dve.wait_ge(turned_done, n + 1)
                for kt in range(KT):
                    o = osum[:, kt, b * PIX:(b + 1) * PIX].rearrange("p (i r w) -> p w r i", i=WS, r=WS)[:, w:w + 4]
                    last = nc.vector.tensor_tensor(o, turned[n % 4][:, :, kt].rearrange("p w (r i) -> p w r i", i=WS),
                                                   o, ALU.add)
                last.then_inc(added, 1)


def mlp_part(nc, x1, osum, projw, fc1w, fc2w, vec, out):
    with ExitStack() as ctx:
        def sb(name, shape, dt=F32):
            return ctx.enter_context(nc.sbuf_tensor("mlp_" + name, shape, dt))

        def sem(name):
            return ctx.enter_context(nc.semaphore("mlp_" + name))

        projw_sb = sb("projw_sb", [P, KT, C])
        fc1w_sb = sb("fc1w_sb", [P, KT, HID])
        fc2w_sb = sb("fc2w_sb", [P, FT, C])
        vec_sb = sb("vec_sb2", [P, NVEC])
        mean_w = sb("mean_w", [P, P])
        eps = sb("eps", [P, 1])
        x_in = sb("x_in", [P, 2, KT, CHUNK])
        xc = sb("xc", [P, KT, CHUNK])
        sq = sb("sq", [P, KT, CHUNK])
        std = sb("std", [P, CHUNK])
        rstd = sb("rstd", [P, CHUNK])
        xh = sb("xh", [P, KT, CHUNK])
        xn = sb("xn", [P, 2, KT, CHUNK])
        x2 = sb("x2", [P, 2, KT, CHUNK])
        hid = sb("hid", [P, FT, CHUNK])
        y = sb("y2", [P, KT, CHUNK])

        def bank(name):
            return ctx.enter_context(nc.psum_tensor("mlp_" + name, [P, 512], F32))

        pj = [bank("pj0"), bank("pj1")]
        sc = [bank("sc0"), bank("sc1")]
        tp = [bank("tp0"), bank("tp1")]
        ob = [bank("ob0"), bank("ob1")]

        weights_landed = sem("weights_landed2")
        setup_done = sem("setup_done")
        x_landed = [sem("xin_landed0"), sem("xin_landed1")]
        mean_done = sem("mean_done")
        centered = sem("centered")
        squared = sem("squared")
        var_done = sem("var_done")
        std_done = sem("std_done")
        rstd_done = sem("rstd_done")
        scaled = sem("scaled")
        xn_ready = sem("xn_ready")
        out_projected = sem("out_projected2")
        x2_ready = sem("x2_ready")
        fc1_done = sem("fc1_done")
        hid_ready = sem("hid_ready")
        fc2_done = sem("fc2_done")
        y_ready = sem("y_ready2")
        y_stored = sem("y_stored2")

        LOADS = 4

        def v(name, kt=0):
            return vec_sb[:, VEC[name] + kt:VEC[name] + kt + 1]

        def o_rows(kt, n):
            return osum[:, kt].rearrange("p (i r s c) -> p i r c s", i=B * CHUNKS, r=WS, s=WS)[
                :, bass.ds(n, 1)].squeeze(1)

        block = ctx.enter_context(nc.Block())


        @block.sync
        def _(sp):
            for dst, src in ((vec_sb[:], vec), (projw_sb[:], projw.rearrange("(k p) o -> p k o", p=P)),
                             (fc1w_sb[:], fc1w.rearrange("(k p) o -> p k o", p=P)),
                             (fc2w_sb[:], fc2w.rearrange("(k p) o -> p k o", p=P))):
                sp.dma_start(dst, src).then_inc(weights_landed, 16)

            def load(b, i, k):
                sp.dma_start(x_in[:, k], x1[b].rearrange("(k p) n -> p k n", p=P)[
                    :, :, bass.ts(i, CHUNK)]).then_inc(x_landed[k], 16)

            def pair(b, i, following):
                for k in range(2):
                    n = b * CHUNKS + 2 * i + k
                    if following:
                        nb, ni = following
                        sp.wait_ge(x2_ready, n + 2)
                        load(nb, 2 * ni + k, k)
                    sp.wait_ge(y_ready, n + 2)
                    sp.dma_start(out[b].rearrange("(k p) n -> p k n", p=P)[:, :, bass.ts(2 * i + k, CHUNK)],
                                 y[:]).then_inc(y_stored, 16)
            load(0, 0, 0)
            load(0, 1, 1)
            for b in range(B):
                with sp.Fori(0, CHUNKS // 2 - 1) as i:
                    pair(b, i, (b, i + 1))
                pair(b, CHUNKS // 2 - 1, (b + 1, 0) if b + 1 < B else None)
            sp.wait_ge(y_stored, 16 * (B * CHUNKS + 1))

        @block.gpsimd
        def _(pool):
            for s in (centered, scaled, xn_ready, x2_ready, y_ready, fc2_done):
                pool.sem_inc(s, 1)
            pool.sem_inc(y_stored, 16)

        @block.tensor
        def _(pe):
            def project(n):
                for ct in range(KT):
                    for kt in range(KT):
                        last = nc.tensor.matmul(pj[ct][:], projw_sb[:, kt, ct * P:(ct + 1) * P],
                                                o_rows(kt, n), start=kt == 0, stop=kt == KT - 1)
                last.then_inc(out_projected, 1)

            def mean(n, k):
                pe.wait_ge(x2_ready, n + 2)
                for kt in range(KT):
                    last = nc.tensor.matmul(pj[0][:], mean_w[:], x2[:, k, kt], start=kt == 0, stop=kt == KT - 1)
                last.then_inc(mean_done, 1)

            def variance(n):
                pe.wait_ge(squared, n + 1)
                for kt in range(KT):
                    last = nc.tensor.matmul(pj[1][:], mean_w[:], sq[:, kt], start=kt == 0, stop=kt == KT - 1)
                last.then_inc(var_done, 1)

            banks = sc + tp

            def chunk(n, k, following):
                def fc1(ft):
                    if ft >= 4:
                        pe.wait_ge(hid_ready, n * FT + ft - 1)
                    for kt in range(KT):
                        last = nc.tensor.matmul(banks[ft % 4][:], fc1w_sb[:, kt, ft * P:(ft + 1) * P],
                                                xn[:, k, kt], start=kt == 0, stop=kt == KT - 1)
                    last.then_inc(fc1_done, 1)

                def fc2(ft):
                    if ft == 0:
                        pe.wait_ge(y_ready, n + 1)
                    pe.wait_ge(hid_ready, n * FT + ft + 3)
                    for ct in range(KT):
                        last = nc.tensor.matmul(ob[ct][:], fc2w_sb[:, ft, ct * P:(ct + 1) * P], hid[:, ft],
                                                start=ft == 0, stop=ft == FT - 1)
                    if ft == FT - 1:
                        last.then_inc(fc2_done, 1)
                pe.wait_ge(xn_ready, n + 2)
                for ft in range(FT):
                    fc1(ft)
                    if following:
                        if ft == 1:
                            project(n + 1)
                        if ft == 3:
                            mean(n + 1, 1 - k)
                        if ft == 5:
                            variance(n + 1)
                    if ft >= 2:
                        fc2(ft - 2)
                fc2(FT - 2)
                fc2(FT - 1)

            pe.wait_ge(weights_landed, 16 * LOADS)
            pe.wait_ge(setup_done, 1)
            project(0)
            mean(0, 0)
            variance(0)
            with pe.Fori(0, B * CHUNKS // 2 - 1) as j:
                for k in range(2):
                    chunk(2 * j + k, k, True)
            chunk(B * CHUNKS - 2, 0, True)
            chunk(B * CHUNKS - 1, 1, False)

        @block.scalar
        def _(act):
            act.sem_inc(hid_ready, 2)
            act.wait_ge(weights_landed, 16 * LOADS)
            act.wait_ge(setup_done, 1)

            def square(n):
                act.wait_ge(centered, n + 2)
                nc.scalar.activation(sq[:], xc[:], ACT.Square).then_inc(squared, 1)

            def deviation(n):
                act.wait_ge(var_done, n + 1)
                nc.scalar.activation(std[:], pj[1][:], ACT.Sqrt, bias=eps[:]).then_inc(std_done, 1)

            def affine(n, k):
                act.wait_ge(scaled, n + 2)
                for kt in range(KT):
                    last = nc.scalar.activation(xn[:, k, kt], xh[:, kt], ACT.Identity, scale=v("norm2_g", kt),
                                                bias=v("norm2_b", kt))
                last.then_inc(xn_ready, 1)

            def chunk(n, k, following):
                for ft in range(FT):
                    act.wait_ge(fc1_done, n * FT + ft + 1)
                    if ft == 0:
                        act.wait_ge(fc2_done, n + 1)
                    nc.scalar.activation(hid[:, ft], (sc + tp)[ft % 4][:], ACT.Gelu,
                                         bias=v("fc1_b", ft)).then_inc(hid_ready, 1)
                    if following:
                        if ft == 2:
                            square(n + 1)
                        if ft == 5:
                            deviation(n + 1)
                        if ft == 6:
                            affine(n + 1, 1 - k)

            square(0)
            deviation(0)
            affine(0, 0)
            with act.Fori(0, B * CHUNKS // 2 - 1) as j:
                for k in range(2):
                    chunk(2 * j + k, k, True)
            chunk(B * CHUNKS - 2, 0, True)
            chunk(B * CHUNKS - 1, 1, False)

        @block.vector
        def _(dve):
            nc.vector.memset(mean_w[:], 1.0 / C)
            nc.vector.memset(eps[:], EPS).then_inc(setup_done, 1)
            dve.wait_ge(weights_landed, 16 * LOADS)

            def norm(n, j, k):
                dve.wait_ge(out_projected, n + 1)
                dve.wait_ge(x_landed[k], 16 * (j + 1))
                for ct in range(KT):
                    last = nc.vector.scalar_tensor_tensor(x2[:, k, ct], pj[ct][:], v("proj_b", ct), x_in[:, k, ct],
                                                          ALU.add, ALU.add)
                last.then_inc(x2_ready, 1)
                dve.wait_ge(mean_done, n + 1)
                dve.wait_ge(scaled, n + 1)
                for kt in range(KT):
                    last = nc.vector.tensor_tensor(xc[:, kt], x2[:, k, kt], pj[0][:], ALU.subtract)
                last.then_inc(centered, 1)
                dve.wait_ge(std_done, n + 1)
                nc.vector.reciprocal(rstd[:], std[:]).then_inc(rstd_done, 1)
                dve.wait_ge(rstd_done, n + 1)
                dve.wait_ge(xn_ready, n + 1)
                for kt in range(KT):
                    last = nc.vector.tensor_tensor(xh[:, kt], xc[:, kt], rstd[:], ALU.mult)
                last.then_inc(scaled, 1)

            def chunk(n, k, following):
                if following is not None:
                    dve.wait_ge(y_ready, n + 1)
                    norm(n + 1, following, 1 - k)
                dve.wait_ge(fc2_done, n + 2)
                dve.wait_ge(y_stored, 16 * n + 16)
                for ct in range(KT):
                    last = nc.vector.scalar_tensor_tensor(y[:, ct], ob[ct][:], v("fc2_b", ct), x2[:, k, ct],
                                                          ALU.add, ALU.add)
                last.then_inc(y_ready, 1)

            norm(0, 0, 0)
            with dve.Fori(0, B * CHUNKS // 2 - 1) as j:
                chunk(2 * j, 0, j)
                chunk(2 * j + 1, 1, j + 1)
            chunk(B * CHUNKS - 2, 0, B * CHUNKS // 2 - 1)
            chunk(B * CHUNKS - 1, 1, None)


def program(nc, x, wqk, bqk, wg, wout, vec, ident, qkvw, bv, rpb, projw, taps, flip, fc1w, fc2w, out):
    x1 = nc.dram_tensor("x1_scratch", (B, C, PIX), F32).ap()
    nonlocal_part(nc, x, wqk, bqk, wg, wout, vec, ident, x1)
    v_img = nc.dram_tensor("v_scratch", (B, 4, H, W, 2 * QC), F32).ap()
    o_att = nc.dram_tensor("o_scratch", (B, CHUNKS, C, CHUNK), F32).ap()
    window_part(nc, x1, qkvw, bv, rpb, vec, ident, v_img, o_att)
    with ExitStack() as ctx:
        gz = ctx.enter_context(nc.sbuf_tensor("gz", [P, P, B * W], F32))
        conv_part(nc, v_img, taps, gz)
        osum = ctx.enter_context(nc.sbuf_tensor("osum", [P, KT, B * PIX], F32))
        turn_part(nc, gz, o_att, flip, osum)
        mlp_part(nc, x1, osum, projw, fc1w, fc2w, vec, out)


def kernel(**inputs):
    import numpy as np
    import concourse.bacc as bacc
    from concourse.bass_utils import run_bass_kernel_spmd

    a = {k: np.asarray(v) for k, v in inputs.items()}
    L0, L1 = "L0_conv_", "L1_conv_"

    def cols(v):
        return v.reshape(-1, P).T

    vec = np.concatenate([cols(v) for v in (
        a[L0 + "b_g"], a[L0 + "b_out"], a[L1 + "norm1_g"], a[L1 + "norm1_b"], a[L1 + "qkv_b"], a[L1 + "proj_b"],
        a[L1 + "gaze_b"], a[L1 + "norm2_g"], a[L1 + "norm2_b"], a[L1 + "fc1_b"], a[L1 + "fc2_b"])], axis=1)
    at = np.stack(np.meshgrid(np.arange(WS), np.arange(WS), indexing="ij")).reshape(2, -1)
    off = at[:, :, None] - at[:, None, :] + WS - 1
    rpb = a[L1 + "rpb_table"][off[0] * (2 * WS - 1) + off[1]]
    rpb = rpb.reshape(WS * WS, WS * WS, HP, 2).transpose(3, 0, 2, 1).reshape(P, HP * WS * WS)
    v_order = np.arange(C).reshape(2, 4, HD).transpose(1, 0, 2).ravel()
    taps = np.zeros((C, 2 * GE, LINE), np.float32)
    taps[:, :GK, H - GK // 2 - 1:H + GK // 2] = a[L1 + "gaze_w"][:, :, 0].transpose(2, 1, 0)
    flip = np.kron(np.eye(KT, dtype=np.float32), np.eye(H, dtype=np.float32)[::-1])
    arrays = {
        "x": a["x"].reshape(B, C, PIX),
        "wqk": np.concatenate([a[L0 + "w_theta"], a[L0 + "w_phi"]]).T,
        "bqk": np.broadcast_to(np.concatenate([a[L0 + "b_theta"], a[L0 + "b_phi"]]), (P, 2 * CH)),
        "wg": a[L0 + "w_g"].T,
        "wout": a[L0 + "w_out"].T,
        "vec": vec,
        "ident": np.eye(P, dtype=np.float32),
        "qkvw": np.concatenate([a[L1 + "qkv_w"][:2 * C], a[L1 + "qkv_w"][2 * C:][v_order]]).T,
        "bv": np.broadcast_to(a[L1 + "qkv_b"][2 * C:][v_order], (P, C)),
        "rpb": rpb,
        "projw": a[L1 + "proj_w"].T,
        "taps": taps,
        "flip": flip,
        "fc1w": a[L1 + "fc1_w"].T,
        "fc2w": a[L1 + "fc2_w"].T,
    }
    nc = bacc.Bacc("TRN2", target_bir_lowering=False, num_devices=1)
    fed, args = {}, []
    for name, v in arrays.items():
        v = np.ascontiguousarray(v)
        fed[f"in_{name}"] = v
        args.append(nc.dram_tensor(f"in_{name}", v.shape, mybir.dt.from_np(v.dtype), kind="ExternalInput").ap())
    args.append(nc.dram_tensor("out_x", (B, C, PIX), F32, kind="ExternalOutput").ap())
    program(nc, *args)
    r = run_bass_kernel_spmd(nc, [fed], core_ids=[0])
    return r.results[0]["out_x"].reshape(B, C, H, W)
```

```python
from contextlib import ExitStack

import concourse.bass as bass
from concourse import mybir

F32 = mybir.dt.float32
BF16 = mybir.dt.bfloat16
ALU = mybir.AluOpType
ACT = mybir.ActivationFunctionType
X = mybir.AxisListType.X

P = 128
B, C, H, W = 2, 256, 64, 64
PIX = H * W
CH = C // 2
KT = C // P
LK = CH * H
HALF = W
CHUNK = 512
ROWS = CHUNK // W
CHUNKS = PIX // CHUNK
GROUP = 512
QT = GROUP // P
GROUPS = LK // GROUP
UNITS = LK // (2 * P)
MAXCH = QT * LK // 512
KCH = LK // 512
TURNS = UNITS // 4 - 1
VX = 2 * W + 1

WS = 8
NH = 8
HD = C // NH
HP = NH // 2
HID = 1024
FT = HID // P
GK = 9
PADW = W + GK - 1
QC = P // 4
GE = (GK + 1) // 2
BANDS = 4
LINE = 128
EPS = 1e-5
SCALE = 4.0

VEC = {}
_n = 0
for _name, _w in (("b_g", 1), ("b_out", KT), ("norm1_g", KT), ("norm1_b", KT), ("qkv_b", 3 * KT), ("proj_b", KT),
                  ("gaze_b", KT), ("norm2_g", KT), ("norm2_b", KT), ("fc1_b", FT), ("fc2_b", KT)):
    VEC[_name] = _n
    _n += _w
NVEC = _n


def nonlocal_part(nc, x, wqk, bqk, wg, wout, vec, ident, x1):
    with ExitStack() as ctx:
        def sb(name, shape, dt=F32):
            return ctx.enter_context(nc.sbuf_tensor(name, shape, dt))

        def sem(name):
            return ctx.enter_context(nc.semaphore(name))

        wqk_sb = sb("wqk_sb", [P, KT, 2 * CH])
        bqk_sb = sb("bqk_sb", [P, 2 * CH])
        wg_sb = sb("wg_sb", [P, KT, CH])
        wout_sb = sb("wout_sb", [P, C])
        vec_sb = sb("vec_sb1", [P, NVEC])
        ident_sb = sb("ident_sb1", [P, P])
        x_ring = sb("x_ring", [P, 2, KT, ROWS, 2, W])
        proj = sb("proj", [P, 2, 2, 2 * CH])
        q1 = sb("q1", [P, LK], BF16)
        q2 = sb("q2", [P, LK], BF16)
        kh = sb("kh", [P, LK], BF16)
        kl = sb("kl", [P, LK], BF16)
        g_sb = sb("g_sb", [P, H, VX], BF16)
        probs = sb("probs", [P, 2, 2 * GROUP])
        p_high = sb("p_high", [P, 4, 2 * GROUP], BF16)
        p_low = sb("p_low", [P, 4, 2 * GROUP], BF16)
        chunk_max = sb("chunk_max", [P, KCH, QT])
        qmax = sb("qmax", [P, QT])
        neg_max = sb("neg_max", [P, QT])
        rden = sb("rden", [P, QT])
        o_high = sb("o_high", [P, QT * W])
        o_low = sb("o_low", [P, QT * W])
        o_grp = sb("o_grp", [P, QT * W])
        x_res = sb("x_res", [P, KT, QT * W])
        y = sb("y", [P, KT, QT * W])

        sT = ctx.enter_context(nc.psum_tensor("sT", [P, 2, 2, 512], F32))
        s_max = ctx.enter_context(nc.psum_tensor("s_max", [P, 2, 512], F32))
        acc = ctx.enter_context(nc.psum_tensor("acc", [P, 2, 512], F32))
        shift_ps, out_ps = s_max[:, 0], s_max[:, 1]

        weights_landed = sem("weights_landed")
        x_landed = [sem("x_landed0"), sem("x_landed1")]
        qk_projected = sem("qk_projected")
        qk_biased = sem("qk_biased")
        high_done = sem("high_done")
        split_done = sem("split_done")
        g_projected = sem("g_projected")
        g_high = sem("g_high")
        g_ready = sem("g_ready")
        ones_ready = sem("ones_ready")
        max_scored = sem("max_scored")
        max_free = sem("max_free")
        qmax_done = sem("qmax_done")
        neg_ready = sem("neg_ready")
        row_done = sem("row_done")
        row_high = sem("row_high")
        shift_ready = sem("shift_ready")
        scored = sem("scored")
        high_ready = sem("high_ready")
        low_ready = sem("low_ready")
        low_ready2 = sem("low_ready2")
        pv_done = sem("pv_done")
        rden_done = sem("rden_done")
        normed = sem("normed")
        out_projected = sem("out_projected")
        res_landed = sem("res_landed")
        y_ready = sem("y_ready")
        y_stored = sem("y_stored")

        LOADS = 6
        SPLIT = 3 * P
        block = ctx.enter_context(nc.Block())

        @block.sync
        def _(sp):
            def load(b, i):
                for k in range(2):
                    sp.wait_ge(g_projected, b * CHUNKS + 2 * i + k + 1)
                    for kt in range(KT):
                        for copy in range(2):
                            sp.dma_start(x_ring[:, k, kt, :, copy], x[b, kt * P:(kt + 1) * P, bass.ts(
                                2 * i + k, CHUNK)].rearrange("p (r w) -> p r w", w=W)).then_inc(x_landed[k], 16)
            load(0, 0)
            for b in range(B):
                with sp.Fori(1, CHUNKS // 2) as i:
                    load(b, i)
                if b + 1 < B:
                    load(b + 1, 0)
                with sp.Fori(0, GROUPS) as g:
                    sp.wait_ge(y_ready, b * GROUPS + g + 1)
                    sp.dma_start(x_res[:], x[b].rearrange("(k p) n -> p k n", p=P)[
                        :, :, bass.ts(g, QT * W)]).then_inc(res_landed, 16)
                    sp.wait_ge(y_ready, b * GROUPS + g + 2)
                    sp.dma_start(x1[b].rearrange("(k p) n -> p k n", p=P)[:, :, bass.ts(g, QT * W)],
                                 y[:]).then_inc(y_stored, 16)
            sp.wait_ge(y_stored, 16 * (B * GROUPS + 1))

        @block.tensor
        def _(pe):
            def score_max(n, t, kc, bank):
                pe.wait_ge(max_free, n + 1)
                nc.tensor.matmul(bank, q1[:, bass.ts(t, P)], kh[:, bass.ts(kc, 512)], start=True,
                                 stop=True).then_inc(max_scored, 1)

            def score_t(unit, g, u, buf, free):
                if free:
                    pe.wait_ge(high_ready, unit - 1)
                qs = bass.ts(g, GROUP)
                for k in range(2):
                    ks = bass.ts(2 * u + k, P)
                    nc.tensor.matmul(sT[:, buf, k], kh[:, ks], q1[:, qs], start=True, stop=False)
                    last = nc.tensor.matmul(sT[:, buf, k], kl[:, ks], q2[:, qs], start=False, stop=True)
                last.then_inc(scored, 1)

            def weigh(unit, u, buf, first=False):
                for k in range(2):
                    for t in range(QT):
                        if k * GROUP + t * P == 0:
                            pe.wait_ge(low_ready, unit + 1)
                        elif k * GROUP + t * P == SPLIT:
                            pe.wait_ge(low_ready2, unit + 1)
                        out = acc[:, t // 2, (t % 2) * VX:(t % 2 + 1) * VX]
                        cols = slice(k * GROUP + t * P, k * GROUP + (t + 1) * P)
                        nc.tensor.matmul(out, p_high[:, buf, cols], g_sb[:, 2 * u + k, :],
                                         start=first and k == 0 and t % 2 == 0, stop=False, skip_group_check=True)
                        last = nc.tensor.matmul(out[:, 0:W + 1], p_low[:, buf, cols], g_sb[:, 2 * u + k, 0:W + 1],
                                                start=False, stop=False, skip_group_check=True)
                last.then_inc(pv_done, 1)

            def shift_rows(grp):
                pe.wait_ge(neg_ready, grp + 2)
                for t in range(QT):
                    last = nc.tensor.matmul(shift_ps[:, t * P:(t + 1) * P], neg_max[:, t:t + 1].to_broadcast([P, P]),
                                            ident_sb[:], start=True, stop=True)
                last.then_inc(row_done, 1)

            def start(grp, g):
                pe.wait_ge(shift_ready, grp + 1)
                score_t(grp * UNITS, g, 0, 0, False)
                score_t(grp * UNITS + 1, g, 1, 1, False)

            def project_out(grp):
                pe.wait_ge(normed, grp + 2)
                for ct in range(KT):
                    last = nc.tensor.matmul(out_ps[:, ct * QT * W:(ct + 1) * QT * W], wout_sb[:, ct * P:(ct + 1) * P],
                                            o_grp[:], start=True, stop=True)
                last.then_inc(out_projected, 1)

            def group(grp, g, first, ahead):
                n0 = (grp + 1) * MAXCH

                def look(c):
                    if ahead:
                        score_max(n0 + c, (g + 1) * QT + c % QT, c // QT, s_max[:, c % 2])

                u0 = grp * UNITS
                if not first:
                    project_out(grp - 1)
                score_t(u0 + 2, g, 2, 0, True)
                pe.wait_ge(y_ready, grp + 1)
                look(0)
                look(1)
                weigh(u0, 0, 0, first=True)
                look(2)
                look(3)
                score_t(u0 + 3, g, 3, 1, True)
                for c in range(4, 8):
                    look(c)
                with pe.Fori(0, TURNS) as i:
                    for j in range(4):
                        u = 4 * i + 2 + j
                        if ahead:
                            for c in (2 * j, 2 * j + 1):
                                score_max(n0 + 8 * i + 8 + c, (g + 1) * QT + c % QT, 2 * i + 2 + c // QT,
                                          s_max[:, c % 2])
                        weigh(u0 + u - 1, u - 1, (j + 1) % 4)
                        score_t(u0 + u + 2, g, u + 2, j % 2, True)
                weigh(u0 + UNITS - 3, UNITS - 3, 1)
                if ahead:
                    shift_rows(grp + 1)
                weigh(u0 + UNITS - 2, UNITS - 2, 2)
                weigh(u0 + UNITS - 1, UNITS - 1, 3)
                if ahead:
                    start(grp + 1, g + 1)

            pe.sem_inc(g_projected, 2)
            pe.wait_ge(weights_landed, 16 * LOADS)
            with pe.Fori(0, B) as b:
                def first_max(c, part):
                    if part == 0:
                        pe.wait_ge(split_done, (b * CHUNKS + c + 1) * 4 + 1)
                    for j in (2 * part, 2 * part + 1):
                        score_max(b * GROUPS * MAXCH + 8 * c + j, j % QT, 2 * c + j // QT, acc[:, j % 2])

                def project(i, k, following):
                    c = 2 * i + k
                    chunk = b * CHUNKS + c
                    pe.wait_ge(x_landed[k], 64 * (b * (CHUNKS // 2) + i) + 64)
                    for hh in range(ROWS // 2):
                        if hh >= 2:
                            pe.wait_ge(qk_biased, chunk * 4 + hh)
                        else:
                            pe.wait_ge(qk_biased, chunk * 4 + 1)
                        for j in range(2):
                            row = 2 * hh + j
                            for kt in range(KT):
                                xs = x_ring[:, k, kt, row].rearrange("p c w -> p (c w)")
                                last = nc.tensor.matmul(sT[:, hh % 2, 0, j * 2 * CH:(j + 1) * 2 * CH], xs,
                                                        wqk_sb[:, kt], start=kt == 0, stop=kt == KT - 1)
                        last.then_inc(qk_projected, 1)
                        if following and hh:
                            first_max(c - 1, hh - 1)
                    if following:
                        first_max(c - 1, 3)
                    pe.wait_ge(g_ready, chunk + 1)
                    for kt in range(KT):
                        last = nc.tensor.matmul(s_max[:, 0], wg_sb[:, kt], x_ring[:, k, kt, :, 0], start=kt == 0,
                                                stop=kt == KT - 1)
                    last.then_inc(g_projected, 1)

                project(0, 0, False)
                project(0, 1, True)
                with pe.Fori(1, CHUNKS // 2) as i:
                    for k in range(2):
                        project(i, k, True)
                for part in range(4):
                    first_max(CHUNKS - 1, part)
                pe.wait_ge(ones_ready, 4)
                pe.wait_ge(g_ready, (b + 1) * CHUNKS + 1)
                pe.wait_ge(y_ready, b * GROUPS + 1)
                shift_rows(b * GROUPS)
                start(b * GROUPS, 0)
                group(b * GROUPS, 0, True, True)
                with pe.Fori(1, GROUPS - 1) as g:
                    group(b * GROUPS + g, g, False, True)
                group(b * GROUPS + GROUPS - 1, GROUPS - 1, False, False)
                project_out(b * GROUPS + GROUPS - 1)

        @block.scalar
        def _(act):
            for dst, src in ((wqk_sb[:], wqk.rearrange("(k p) o -> p k o", p=P)), (bqk_sb[:], bqk),
                             (wg_sb[:], wg.rearrange("(k p) o -> p k o", p=P)), (wout_sb[:], wout),
                             (vec_sb[:], vec), (ident_sb[:], ident)):
                act.dma_start(dst, src).then_inc(weights_landed, 16)
            act.wait_ge(weights_landed, 16 * LOADS)

            def exponent(unit, buf, reused, reused_high):
                act.wait_ge(scored, unit + 1)
                if reused:
                    act.wait_ge(low_ready, unit - 1)
                    act.wait_ge(low_ready2, unit - 1)
                src = sT[:, buf % 2].rearrange("p k n -> p (k n)")
                nc.scalar.activation(probs[:, buf % 2], src, ACT.Exp)
                if reused_high:
                    act.wait_ge(pv_done, unit - 3)
                nc.scalar.activation(p_high[:, buf], src, ACT.Exp).then_inc(high_ready, 1)

            with act.Fori(0, B) as b:
                with act.Fori(0, CHUNKS) as c:
                    chunk = b * CHUNKS + c
                    for hh in range(ROWS // 2):
                        act.wait_ge(qk_biased, chunk * 4 + hh + 2)
                        pr = proj[:, hh % 2]
                        cols = bass.ds(c * ROWS * CH + hh * 2 * CH, 2 * CH)

                        def two(t, lo=0, hi=P):
                            return t[lo:hi, cols].rearrange("p (r o) -> p r o", r=2)
                        nc.scalar.activation(two(q1), pr[:, :, 0:CH], ACT.Identity)
                        nc.scalar.activation(two(kh), pr[:, :, CH:2 * CH], ACT.Identity)
                        nc.scalar.activation(two(q2, 0, HALF), pr[0:HALF, :, 0:CH], ACT.Identity).then_inc(high_done, 1)
                    act.wait_ge(g_projected, chunk + 3)
                    nc.scalar.activation(g_sb[:, bass.ts(c, ROWS), 0:W], s_max[:, 0].rearrange("p (r w) -> p r w", w=W),
                                         ACT.Identity, bias=vec_sb[:, VEC["b_g"]:VEC["b_g"] + 1]).then_inc(g_high, 1)
                with act.Fori(0, GROUPS) as g:
                    u0 = (b * GROUPS + g) * UNITS
                    for u in range(4):
                        exponent(u0 + u, u, u >= 2, False)
                    with act.Fori(0, TURNS) as i:
                        for k in range(4):
                            exponent(u0 + 4 * i + 4 + k, k, True, True)

        @block.gpsimd
        def _(pool):
            for s in (qk_biased, split_done, g_ready, normed, neg_ready, y_ready):
                pool.sem_inc(s, 1)
            pool.sem_inc(y_stored, 16)
            nc.gpsimd.memset(kl[HALF:P, :].bitcast(F32), 0.0).then_inc(ones_ready, 1)
            pool.wait_ge(ones_ready, 1)
            nc.gpsimd.memset(kl[HALF:HALF + 1, :], 1.0).then_inc(ones_ready, 1)
            nc.gpsimd.memset(kl[HALF + 32:HALF + 33, :], 1.0).then_inc(ones_ready, 1)
            pool.wait_ge(ones_ready, 3)
            nc.gpsimd.memset(g_sb[:, :, W:W + 1], 1.0).then_inc(ones_ready, 1)
            with pool.Fori(0, B * GROUPS * UNITS // 4) as i:
                for buf in range(4):
                    pool.wait_ge(high_ready, 4 * i + buf + 1)
                    nc.gpsimd.tensor_tensor(p_low[:, buf, SPLIT:], probs[:, buf % 2, SPLIT:], p_high[:, buf, SPLIT:],
                                            ALU.subtract).then_inc(low_ready2, 1)

        @block.vector
        def _(dve):
            def maximum(n0, c, bank):
                dve.wait_ge(max_scored, n0 + c + 1)
                nc.vector.tensor_reduce(chunk_max_flat[:, bass.ds(c, 1)], bank, X,
                                        ALU.max).then_inc(max_free, 1)

            def low_probs(unit, buf):
                dve.wait_ge(high_ready, unit + 1)
                nc.vector.tensor_tensor(p_low[:, buf, 0:SPLIT], probs[:, buf % 2, 0:SPLIT], p_high[:, buf, 0:SPLIT],
                                        ALU.subtract).then_inc(low_ready, 1)

            def negate(grp):
                dve.wait_ge(max_free, 2 + (grp + 1) * MAXCH)
                dve.wait_ge(neg_ready, grp + 1)
                nc.vector.tensor_reduce(qmax[:], chunk_max[:].rearrange("p k t -> p t k"), X, ALU.max).then_inc(qmax_done, 1)
                dve.wait_ge(qmax_done, grp + 1)
                nc.vector.tensor_scalar(neg_max[:], qmax[:], -1.0, None, ALU.mult).then_inc(neg_ready, 1)

            def write_shift_high(grp, g):
                dve.wait_ge(row_done, grp + 1)
                nc.vector.tensor_copy(q2[HALF:P, bass.ts(g, GROUP)], shift_ps[HALF:P, :]).then_inc(row_high, 1)

            def write_shift_low(grp, g):
                cols = bass.ts(g, GROUP)
                dve.wait_ge(row_high, grp + 1)
                nc.vector.tensor_tensor(q2[HALF + 32:P, cols], shift_ps[HALF + 32:P, :], q2[HALF + 32:P, cols],
                                        ALU.subtract).then_inc(shift_ready, 1)

            def residual(grp):
                dve.wait_ge(out_projected, grp + 1)
                dve.wait_ge(res_landed, 16 * (grp + 1))
                dve.wait_ge(y_stored, 16 * grp + 16)
                for ct in range(KT):
                    last = nc.vector.scalar_tensor_tensor(
                        y[:, ct], out_ps[:, ct * QT * W:(ct + 1) * QT * W],
                        vec_sb[:, VEC["b_out"] + ct:VEC["b_out"] + ct + 1], x_res[:, ct], ALU.add, ALU.add)
                last.then_inc(y_ready, 1)

            def group(grp, g, first, ahead):
                n0 = (grp + 1) * MAXCH
                u0 = grp * UNITS

                def look(c, buf):
                    if ahead:
                        maximum(n0, c, s_max[:, buf])
                if not first:
                    residual(grp - 1)
                low_probs(u0, 0)
                for c in range(4):
                    look(c, c % 2)
                low_probs(u0 + 1, 1)
                for c in range(4, 8):
                    look(c, c % 2)
                with dve.Fori(0, TURNS) as i:
                    for j in range(4):
                        for c in (2 * j, 2 * j + 1):
                            look(8 * i + 8 + c, c % 2)
                        low_probs(u0 + 4 * i + 2 + j, (j + 2) % 4)
                if ahead:
                    negate(grp + 1)
                low_probs(u0 + UNITS - 2, 2)
                if ahead:
                    write_shift_high(grp + 1, g + 1)
                low_probs(u0 + UNITS - 1, 3)
                if ahead:
                    write_shift_low(grp + 1, g + 1)
                dve.wait_ge(pv_done, (grp + 1) * UNITS)
                outs = acc[:, :, 0:2 * VX].rearrange("p b (t w) -> p b t w", t=2)

                def tiles(a):
                    return a.rearrange("p (b t w) -> p b t w", b=2, t=2)
                for bank in range(2):
                    last = nc.vector.reciprocal(rden[:, 2 * bank:2 * bank + 2].unsqueeze(2), outs[:, bank, :, W:W + 1])
                last.then_inc(rden_done, 1)
                dve.wait_ge(rden_done, 3 * grp + 1)
                scale = tiles(rden[:]).to_broadcast([P, 2, 2, W])
                nc.vector.tensor_tensor(tiles(o_low[:]), outs[:, :, :, W + 1:VX], scale, ALU.mult).then_inc(rden_done, 1)
                nc.vector.tensor_tensor(tiles(o_high[:]), outs[:, :, :, 0:W], scale, ALU.mult).then_inc(rden_done, 1)
                dve.wait_ge(rden_done, 3 * grp + 3)
                nc.vector.tensor_tensor(o_grp[:], o_high[:], o_low[:], ALU.add).then_inc(normed, 1)

            chunk_max_flat = chunk_max[:].rearrange("p k t -> p (k t)")
            dve.wait_ge(weights_landed, 16 * LOADS)
            nc.vector.memset(chunk_max[:, 0], 0.0).then_inc(max_free, 1)
            nc.vector.memset(chunk_max[:, 1], 0.0).then_inc(max_free, 1)
            with dve.Fori(0, B) as b:
                def first_max(c, part):
                    for j in (2 * part, 2 * part + 1):
                        maximum(b * GROUPS * MAXCH, 8 * c + j, acc[:, j % 2])

                def split(c, following):
                    chunk = b * CHUNKS + c

                    def bias(hh):
                        dve.wait_ge(split_done, chunk * 4 + (hh if hh >= 2 else 1))
                        dve.wait_ge(qk_projected, chunk * 4 + hh + 1)
                        nc.vector.tensor_tensor(proj[:, hh % 2], sT[:, hh % 2, 0].rearrange("p (r o) -> p r o", r=2),
                                                bqk_sb[:].unsqueeze(1).to_broadcast([P, 2, 2 * CH]),
                                                ALU.add).then_inc(qk_biased, 1)

                    def low(hh):
                        dve.wait_ge(high_done, chunk * 4 + hh + 1)
                        cols = bass.ds(c * ROWS * CH + hh * 2 * CH, 2 * CH)
                        pr = proj[:, hh % 2]
                        ql = q1[HALF:P, cols].rearrange("p (r o) -> p r o", r=2)
                        nc.vector.tensor_tensor(ql, pr[HALF:P, :, 0:CH], ql, ALU.subtract)
                        nc.vector.tensor_tensor(kl[0:HALF, cols].rearrange("p (r o) -> p r o", r=2),
                                                pr[0:HALF, :, CH:2 * CH],
                                                kh[0:HALF, cols].rearrange("p (r o) -> p r o", r=2),
                                                ALU.subtract).then_inc(split_done, 1)
                    bias(0)
                    bias(1)
                    low(0)
                    for hh in range(1, 4):
                        if following:
                            first_max(c - 1, hh - 1)
                        if hh + 1 < 4:
                            bias(hh + 1)
                        low(hh)
                    if following:
                        first_max(c - 1, 3)
                    dve.wait_ge(g_high, chunk + 1)
                    rows = g_sb[:, bass.ts(c, ROWS)]
                    nc.vector.scalar_tensor_tensor(rows[:, :, W + 1:VX], s_max[:, 0].rearrange("p (r w) -> p r w", w=W),
                                                   vec_sb[:, VEC["b_g"]:VEC["b_g"] + 1], rows[:, :, 0:W],
                                                   ALU.add, ALU.subtract).then_inc(g_ready, 1)
                split(0, False)
                with dve.Fori(1, CHUNKS) as c:
                    split(c, True)
                for part in range(4):
                    first_max(CHUNKS - 1, part)
                negate(b * GROUPS)
                write_shift_high(b * GROUPS, 0)
                write_shift_low(b * GROUPS, 0)
                group(b * GROUPS, 0, True, True)
                with dve.Fori(1, GROUPS - 1) as g:
                    group(b * GROUPS + g, g, False, True)
                group(b * GROUPS + GROUPS - 1, GROUPS - 1, False, False)
                residual(b * GROUPS + GROUPS - 1)


def load_band(engine, taps, band, band_landed, n, s):
    for kt in range(KT):
        for half in range(2):
            line = taps[bass.ds(kt * P + n * 4, 1), half, 0:1]
            src = bass.AP(tensor=line.tensor, offset=line.offset, ap=[[1, H], [2 * LINE, 4 * GE], [1, H]])
            engine.dma_start(band[64 * half:64 * half + 64, s, kt].rearrange("p c e h -> p (c e) h"),
                             src).then_inc(band_landed[s], 16)


def window_part(nc, x1, qkvw, bv, rpb, vec, ident, v_img, o_att, taps, band, band_landed):
    with ExitStack() as ctx:
        def sb(name, shape, dt=F32):
            return ctx.enter_context(nc.sbuf_tensor("window_" + name, shape, dt))

        def sem(name):
            return ctx.enter_context(nc.semaphore("window_" + name))

        PAIRS = CHUNK // P

        qkvw_sb = sb("qkvw_sb", [P, KT, 3 * C])
        bv_sb = sb("bv_sb", [P, C])
        rpb_sb = sb("rpb_sb", [P, HP * WS * WS])
        vec_sb = sb("vec_sb2", [P, NVEC])
        ident_sb = sb("ident_sb2", [P, P])
        mean_w = sb("mean_w", [P, P])
        eps = sb("eps", [P, 1])
        x_in = sb("x_in", [P, 2, KT, CHUNK])
        xc = sb("xc", [P, KT, CHUNK])
        sq = sb("sq", [P, KT, CHUNK])
        std = sb("std", [P, CHUNK])
        rstd = sb("rstd", [P, CHUNK])
        xh = sb("xh", [P, KT, CHUNK])
        xn = sb("xn", [P, KT, CHUNK])
        qm = sb("qm", [P, KT, 2, W // WS, 2, WS * WS])
        qb4 = sb("qb4", [P, KT])
        k_sb = sb("k_sb", [P, KT, CHUNK])
        vt = sb("vt", [P, 2, 4, C])
        att = sb("att", [P, PAIRS, CHUNK])
        amax = sb("amax", [P, PAIRS, NH])
        den = sb("den", [P, PAIRS, NH])
        rden = sb("rden2", [P, PAIRS, NH])
        attT = sb("attT", [P, 2, CHUNK])
        o_sb = sb("o_sb", [P, 2, KT, CHUNK])

        def bank(name):
            return ctx.enter_context(nc.psum_tensor("window_" + name, [P, 512], F32))

        pj = [bank("pj0"), bank("pj1")]
        sc = [bank("sc0"), bank("sc1")]
        tp = [bank("tp0"), bank("tp1")]
        ob = [bank("ob0"), bank("ob1")]

        weights_landed = sem("weights_landed2")
        setup_done = sem("setup_done")
        x_landed = [sem("xin_landed0"), sem("xin_landed1")]
        mean_done = sem("mean_done")
        centered = sem("centered")
        squared = sem("squared")
        var_done = sem("var_done")
        std_done = sem("std_done")
        rstd_done = sem("rstd_done")
        scaled = sem("scaled")
        xn_ready = sem("xn_ready")
        projected = sem("projected")
        q_ready = [sem("q_ready0"), sem("q_ready1")]
        k_ready = [sem("k_ready0"), sem("k_ready1")]
        vt_ready = sem("vt_ready")
        att_scored = sem("att_scored")
        att_biased = sem("att_biased")
        amax_done = sem("amax_done")
        shifted = sem("shifted")
        exped = sem("exped")
        den_done = sem("den_done")
        rden_done = sem("rden_done2")
        att_ready = sem("att_ready")
        transposed = sem("transposed")
        attT_ready = sem("attT_ready")
        weighing = sem("weighing")
        attended = sem("attended")
        o_copied = sem("o_copied")
        v_stored = [sem("v_stored0"), sem("v_stored1")]
        o_stored = [sem("o_stored0"), sem("o_stored1")]

        LOADS = 5
        SLOTS = 6
        TILES = B * CHUNKS

        def v(name, kt=0):
            return vec_sb[:, VEC[name] + kt:VEC[name] + kt + 1]

        def win(t):
            return t.rearrange("p (c r s) -> p r c s", c=W // WS, r=WS)

        def v_col(h):
            return (2 * (h % 4) + h // 4) * HD

        def qm_head(rows, kt, r):
            return qm[rows, kt, r // 2, :, r % 2, :]

        block = ctx.enter_context(nc.Block())


        @block.sync
        def _(sp):
            for dst, src in ((vec_sb[:], vec), (qkvw_sb[:], qkvw.rearrange("(k p) o -> p k o", p=P)), (bv_sb[:], bv),
                             (rpb_sb[:], rpb), (ident_sb[:], ident)):
                sp.dma_start(dst, src).then_inc(weights_landed, 16)

            def load(b, i, k):
                sp.dma_start(x_in[:, k], x1[b].rearrange("(k p) n -> p k n", p=P)[
                    :, :, bass.ts(i, CHUNK)]).then_inc(x_landed[k], 16)

            def pair(b, i, following):
                for k in range(2):
                    n = b * CHUNKS + 2 * i + k
                    if following:
                        sp.wait_ge(centered, n + 2)
                        load(following[0], 2 * following[1] + k, k)
                    sp.wait_ge(vt_ready, n * 2 + 4)
                    rows = v_img[b].rearrange("q (r i) (s c) n -> i c r s q n", i=WS, c=WS)[bass.ds(2 * i + k, 1)]
                    for c in range(W // WS):
                        half = slice(64 * (c % 2), 64 * (c % 2) + 64)
                        for q in range(4):
                            sp.dma_start(rows[0, c, :, :, q], vt[half, k, c // 2, 64 * q:64 * q + 64]).then_inc(
                                v_stored[k], 16)
            load(0, 0, 0)
            load(0, 1, 1)
            for s in range(BANDS):
                load_band(sp, taps, band, band_landed, s, s)
            for b in range(B):
                with sp.Fori(0, CHUNKS // 2 - 1) as i:
                    pair(b, i, (b, i + 1))
                pair(b, CHUNKS // 2 - 1, (b + 1, 0) if b + 1 < B else None)
            for k in range(2):
                sp.wait_ge(v_stored[k], 16 * 32 * (TILES // 2) + 1)
                sp.wait_ge(o_stored[k], 16 * (TILES // 2) + 1)

        @block.gpsimd
        def _(pool):
            for s, free in ((centered, 1), (scaled, 1), (xn_ready, 1), (vt_ready, 2), (o_copied, 1), (att_biased, 2),
                            (transposed, PAIRS), (attT_ready, 2), (attended, 2), (v_stored[0], 1), (v_stored[1], 1),
                            (o_stored[0], 1), (o_stored[1], 1)):
                pool.sem_inc(s, free)
            with pool.Fori(0, TILES) as n:
                def subtract(p):
                    pool.wait_ge(amax_done, n * PAIRS + p + 1)
                    a = att[:, p].rearrange("p (g m) -> p g m", g=NH)
                    nc.gpsimd.tensor_tensor(a, a, amax[:, p].unsqueeze(2).to_broadcast([P, NH, WS * WS]),
                                            ALU.subtract).then_inc(shifted, 1)

                def normalise(p):
                    pool.wait_ge(rden_done, n * PAIRS + p + 1)
                    a = att[:, p].rearrange("p (g m) -> p g m", g=NH)
                    nc.gpsimd.tensor_tensor(a, a, rden[:, p].unsqueeze(2).to_broadcast([P, NH, WS * WS]),
                                            ALU.mult).then_inc(att_ready, 1)
                subtract(0)
                for p in range(1, PAIRS):
                    subtract(p)
                    normalise(p - 1)
                normalise(PAIRS - 1)

        @block.tensor
        def _(pe):
            def mean(j, k):
                pe.wait_ge(x_landed[k], 16 * (j + 1))
                for kt in range(KT):
                    last = nc.tensor.matmul(pj[0][:], mean_w[:], x_in[:, k, kt], start=kt == 0, stop=kt == KT - 1)
                last.then_inc(mean_done, 1)

            def variance(n):
                pe.wait_ge(squared, n + 1)
                for kt in range(KT):
                    last = nc.tensor.matmul(pj[1][:], mean_w[:], sq[:, kt], start=kt == 0, stop=kt == KT - 1)
                last.then_inc(var_done, 1)

            def qkv(n):
                def project(bank, col):
                    for kt in range(KT):
                        last = nc.tensor.matmul(bank[:], qkvw_sb[:, kt, col:col + P], xn[:, kt],
                                                start=kt == 0, stop=kt == KT - 1)
                    last.then_inc(projected, 1)
                pe.wait_ge(xn_ready, n + 2)
                for ct in range(KT):
                    project(pj[ct], ct * P)
                for ct in range(KT):
                    project(tp[ct], C + ct * P)
                for h in range(2):
                    pe.wait_ge(q_ready[h], n + 1)
                    for p in range(2):
                        t = (2 * h + p) * P
                        for kt in range(KT):
                            last = nc.tensor.matmul(pj[h][:, p * C:(p + 1) * C], xn[:, kt, t:t + P],
                                                    qkvw_sb[:, kt, 2 * C:3 * C], start=kt == 0, stop=kt == KT - 1)
                    last.then_inc(projected, 1)

            def scores(n, p):
                pe.wait_ge(att_biased, n * PAIRS + p + 1)
                for w in range(2):
                    t = p * P + w * WS * WS
                    for hp in range(HP):
                        lhsT = qm[:, hp // 2, hp % 2, 2 * p + w].rearrange("p b t -> p (b t)")
                        last = nc.tensor.matmul(sc[p % 2][:, (2 * hp + w) * 64:(2 * hp + w + 1) * 64], lhsT,
                                                k_sb[:, hp // 2, t:t + WS * WS], start=True, stop=True)
                last.then_inc(att_scored, 1)

            def turn(n, p):
                pe.wait_ge(att_ready, n * PAIRS + p + 1)
                pe.wait_ge(attT_ready, n * PAIRS + p + 1)
                for hp in range(HP):
                    last = nc.tensor.transpose(tp[p % 2][:, hp * P:(hp + 1) * P], att[:, p, hp * P:(hp + 1) * P], ident_sb[:])
                last.then_inc(transposed, 1)

            def weigh(n, k, p):
                pe.wait_ge(attT_ready, n * PAIRS + p + 3)
                if p == 0:
                    pe.wait_ge(o_copied, n + 1)
                pe.sem_inc(weighing, 1)
                for w in range(2):
                    for h in range(NH):
                        r = h % 4
                        col = (p * KT + h // 4) * 64
                        last = nc.tensor.matmul(ob[w][32 * r:32 * r + 32, col:col + 64],
                                                vt[64 * w:64 * w + 64, k, p, v_col(h):v_col(h) + HD],
                                                attT[64 * w:64 * w + 64, p % 2, h * 64:(h + 1) * 64],
                                                start=True, stop=True)
                last.then_inc(attended, 1)

            def chunk(n, k, following):
                for ct in range(KT):
                    pe.wait_ge(q_ready[ct], n + 1)
                    pe.wait_ge(k_ready[ct], n + 1)
                scores(n, 0)
                scores(n, 1)
                pe.wait_ge(vt_ready, n * 2 + 4)
                if following is not None:
                    mean(following, 1 - k)
                scores(n, 2)
                scores(n, 3)
                if following is not None:
                    variance(n + 1)
                turn(n, 0)
                turn(n, 1)
                weigh(n, k, 0)
                turn(n, 2)
                weigh(n, k, 1)
                turn(n, 3)
                weigh(n, k, 2)
                weigh(n, k, 3)
                if following is not None:
                    qkv(n + 1)

            pe.wait_ge(weights_landed, 16 * LOADS)
            pe.wait_ge(setup_done, 3)
            mean(0, 0)
            variance(0)
            qkv(0)
            with pe.Fori(0, TILES // 2 - 1) as j:
                chunk(2 * j, 0, j)
                chunk(2 * j + 1, 1, j + 1)
            chunk(TILES - 2, 0, TILES // 2 - 1)
            chunk(TILES - 1, 1, None)

        @block.scalar
        def _(act):
            def square(n):
                act.wait_ge(centered, n + 2)
                nc.scalar.activation(sq[:], xc[:], ACT.Square).then_inc(squared, 1)

            def deviation(n):
                act.wait_ge(var_done, n + 1)
                nc.scalar.activation(std[:], pj[1][:], ACT.Sqrt, bias=eps[:]).then_inc(std_done, 1)

            def affine(n):
                act.wait_ge(scaled, n + 2)
                for kt in range(KT):
                    last = nc.scalar.activation(win(xn[:, kt]), xh[:, kt].rearrange("p (r c s) -> p r c s", r=WS, s=WS),
                                                ACT.Identity, scale=v("norm1_g", kt), bias=v("norm1_b", kt))
                last.then_inc(xn_ready, 1)

            def queries_keys(n):
                act.wait_ge(projected, n * SLOTS + 1)
                for r in range(4):
                    rows = slice(32 * r, 32 * r + 32)
                    last = nc.scalar.activation(qm_head(rows, 0, r), pj[0][rows, :].rearrange(
                        "p (c t) -> p c t", c=WS), ACT.Identity, scale=SCALE, bias=qb4[rows, 0:1])
                last.then_inc(q_ready[0], 1)
                act.wait_ge(projected, n * SLOTS + 3)
                nc.scalar.activation(k_sb[:, 0], tp[0][:], ACT.Identity, bias=v("qkv_b", 2)).then_inc(k_ready[0], 1)

            def exponent(n, p):
                act.wait_ge(shifted, n * PAIRS + p + 1)
                nc.scalar.activation(att[:, p], att[:, p], ACT.Exp).then_inc(exped, 1)

            def copy_turned(n, p):
                act.wait_ge(transposed, n * PAIRS + p + PAIRS + 1)
                act.wait_ge(attended, n * PAIRS + p + 1)
                nc.scalar.activation(attT[:, p % 2], tp[p % 2][:], ACT.Identity).then_inc(attT_ready, 1)

            def outputs(n, j, k):
                act.wait_ge(attended, (n + 1) * PAIRS + 2)
                act.wait_ge(o_stored[k], 16 * j + 1)
                for w in range(2):
                    for kt in range(KT):
                        src = ob[w][:].rearrange("p (q k r s) -> p k q r s", k=KT, r=WS, s=WS)[:, kt]
                        dst = o_sb[:, k, kt].rearrange("p (r s q w) -> p w q r s", r=WS, s=WS, w=2)[:, w]
                        last = nc.scalar.activation(dst, src, ACT.Identity, bias=v("gaze_b", kt))
                last.then_inc(o_copied, 1)
                act.wait_ge(o_copied, n + 2)
                act.dma_start(o_att.rearrange("b i (k p) n -> (b i) p k n", p=P)[bass.ds(n, 1)].squeeze(0),
                              o_sb[:, k]).then_inc(o_stored[k], 16)

            def chunk(n, j, k, following):
                exponent(n, 0)
                exponent(n, 1)
                if following:
                    square(n + 1)
                exponent(n, 2)
                copy_turned(n, 0)
                exponent(n, 3)
                if following:
                    deviation(n + 1)
                copy_turned(n, 1)
                copy_turned(n, 2)
                copy_turned(n, 3)
                if following:
                    affine(n + 1)
                outputs(n, j, k)
                if following:
                    queries_keys(n + 1)

            act.wait_ge(weights_landed, 16 * LOADS)
            act.wait_ge(setup_done, 3)
            square(0)
            deviation(0)
            affine(0)
            queries_keys(0)
            with act.Fori(0, TILES // 2 - 1) as j:
                for k in range(2):
                    chunk(2 * j + k, j, k, True)
            chunk(TILES - 2, TILES // 2 - 1, 0, True)
            chunk(TILES - 1, TILES // 2 - 1, 1, False)

        @block.vector
        def _(dve):
            def center(n, k):
                dve.wait_ge(mean_done, n + 1)
                dve.wait_ge(scaled, n + 1)
                for kt in range(KT):
                    last = nc.vector.tensor_tensor(xc[:, kt], x_in[:, k, kt], pj[0][:], ALU.subtract)
                last.then_inc(centered, 1)

            def scale(n):
                dve.wait_ge(std_done, n + 1)
                nc.vector.reciprocal(rstd[:], std[:]).then_inc(rstd_done, 1)
                dve.wait_ge(rstd_done, n + 1)
                dve.wait_ge(xn_ready, n + 1)
                for kt in range(KT):
                    last = nc.vector.tensor_tensor(xh[:, kt], xc[:, kt], rstd[:], ALU.mult)
                last.then_inc(scaled, 1)

            def queries_keys_values(n, j, k):
                dve.wait_ge(projected, n * SLOTS + 2)
                for r in range(4):
                    rows = slice(32 * r, 32 * r + 32)
                    last = nc.vector.tensor_scalar(qm_head(rows, 1, r), pj[1][rows, :].rearrange(
                        "p (c t) -> p c t", c=WS), SCALE, qb4[rows, 1:2], ALU.mult, ALU.add)
                last.then_inc(q_ready[1], 1)
                dve.wait_ge(projected, n * SLOTS + 4)
                nc.vector.tensor_scalar(k_sb[:, 1], tp[1][:], v("qkv_b", 3), None, ALU.add).then_inc(k_ready[1], 1)
                dve.wait_ge(v_stored[k], 16 * 32 * j + 1)
                for h in range(2):
                    dve.wait_ge(projected, n * SLOTS + 5 + h)
                    nc.vector.tensor_tensor(vt[:, k, 2 * h:2 * h + 2], pj[h][:].rearrange("p (q c) -> p q c", q=2),
                                            bv_sb[:].unsqueeze(1).to_broadcast([P, 2, C]),
                                            ALU.add).then_inc(vt_ready, 1)

            def by_window(a):
                return a.rearrange("p (h w m) -> p h w m", h=HP, w=2)

            def bias_and_max(n, p):
                dve.wait_ge(att_scored, n * PAIRS + p + 1)
                dve.wait_ge(transposed, n * PAIRS + p + 1)
                nc.vector.tensor_tensor(by_window(att[:, p]), by_window(sc[p % 2][:]),
                                        rpb_sb[:].rearrange("p (h m) -> p h m", h=HP).unsqueeze(2)
                                        .to_broadcast([P, HP, 2, WS * WS]), ALU.add).then_inc(att_biased, 1)
                dve.wait_ge(att_biased, n * PAIRS + p + 3)
                nc.vector.tensor_reduce(amax[:, p], att[:, p].rearrange("p (g m) -> p g m", g=NH),
                                        X, ALU.max).then_inc(amax_done, 1)

            def denominators(n, p):
                dve.wait_ge(exped, n * PAIRS + p + 1)
                nc.vector.tensor_reduce(den[:, p], att[:, p].rearrange("p (g m) -> p g m", g=NH),
                                        X, ALU.add).then_inc(den_done, 1)
                dve.wait_ge(den_done, n * PAIRS + p + 1)
                nc.vector.reciprocal(rden[:, p], den[:, p]).then_inc(rden_done, 1)

            def chunk(n, k, following):
                bias_and_max(n, 0)
                bias_and_max(n, 1)
                denominators(n, 0)
                if following is not None:
                    center(n + 1, 1 - k)
                bias_and_max(n, 2)
                denominators(n, 1)
                bias_and_max(n, 3)
                denominators(n, 2)
                denominators(n, 3)
                if following is not None:
                    scale(n + 1)
                    queries_keys_values(n + 1, following, 1 - k)

            nc.vector.memset(mean_w[:], 1.0 / C)
            nc.vector.memset(eps[:], EPS).then_inc(setup_done, 1)
            nc.vector.memset(qm[:], 0.0).then_inc(setup_done, 1)
            dve.wait_ge(weights_landed, 16 * LOADS)
            nc.vector.tensor_scalar(qb4[:], vec_sb[:, VEC["qkv_b"]:VEC["qkv_b"] + KT], SCALE, None,
                                    ALU.mult).then_inc(setup_done, 1)
            dve.wait_ge(setup_done, 3)
            center(0, 0)
            scale(0)
            queries_keys_values(0, 0, 0)
            with dve.Fori(0, TILES // 2 - 1) as j:
                chunk(2 * j, 0, j)
                chunk(2 * j + 1, 1, j + 1)
            chunk(TILES - 2, 0, TILES // 2 - 1)
            chunk(TILES - 1, 1, None)


def conv_part(nc, v_img, taps, band, band_landed, gz):
    with ExitStack() as ctx:
        def sb(name, shape, dt=F32):
            return ctx.enter_context(nc.sbuf_tensor("conv_" + name, shape, dt))

        def sem(name):
            return ctx.enter_context(nc.semaphore("conv_" + name))

        v_sb = sb("v_sb", [P, 2, B, PADW, 2 * QC])
        v_ch = sb("v_ch", [P, 2, KT, 4, B, PADW])
        conv = [ctx.enter_context(nc.psum_tensor(f"conv{k}", [P, 4, B * W], F32)) for k in range(2)]

        padding_done = sem("padding_done")
        v_landed = [sem("v_landed0"), sem("v_landed1")]
        v_split = sem("v_split")
        convolving = sem("convolving")
        convolved = sem("convolved")
        gz_copied = sem("gz_copied")

        PERQ = QC // 4
        GROUPS8 = 4 * PERQ

        block = ctx.enter_context(nc.Block())

        @block.sync
        def _(sp):
            with sp.Fori(1, GROUPS8 // BANDS) as t:
                for s in range(BANDS):
                    sp.wait_ge(convolved, t * BANDS + s + 1)
                    load_band(sp, taps, band, band_landed, t * BANDS + s, s)

        @block.gpsimd
        def _(pool):
            for s, n in ((convolved, BANDS), (gz_copied, 2)):
                pool.sem_inc(s, n)
            for k in range(2):
                for b in range(B):
                    for n, cols in enumerate((slice(0, GK // 2), slice(W + GK // 2 - 1, PADW))):
                        if k or b or n:
                            pool.wait_ge(padding_done, 2 * (B * k + b) + n)
                        nc.gpsimd.memset(v_sb[:, k, b, cols], 0.0).then_inc(padding_done, 1)

        @block.scalar
        def _(act):
            def load(q):
                for b in range(B):
                    for half in range(2):
                        at = GK // 2 - half
                        act.dma_start(v_sb[64 * half:64 * half + 64, q % 2, b, at:at + W],
                                      v_img[b, q]).then_inc(v_landed[q % 2], 16)
            act.wait_ge(padding_done, 2 * B)
            load(0)
            act.wait_ge(padding_done, 4 * B)
            load(1)
            for q in range(4):
                act.wait_ge(v_landed[q % 2], 64 * (q // 2 + 1))
                with act.Fori(0, PERQ // 2) as j:
                    for s in range(2):
                        act.wait_ge(convolved, q * PERQ + 2 * j + s + BANDS - 1)
                        for kt in range(KT):
                            src = v_sb[:, q % 2, :, :, kt * QC:(kt + 1) * QC].rearrange("p b w c -> p c (b w)")
                            last = nc.scalar.activation(v_ch[:, s, kt].rearrange("p c b w -> p c (b w)"),
                                                        src[:, bass.ds(8 * j + 4 * s, 4)], ACT.Identity)
                        last.then_inc(v_split, 1)
                if q + 2 < 4:
                    act.wait_ge(v_split, (q + 1) * PERQ)
                    load(q + 2)

        @block.tensor
        def _(pe):
            with pe.Fori(0, GROUPS8 // BANDS) as t:
                for s in range(BANDS):
                    n = t * BANDS + s
                    pe.wait_ge(band_landed[s], 64 * t + 64)
                    pe.wait_ge(v_split, n + 1)
                    pe.wait_ge(gz_copied, n + 1)
                    pe.sem_inc(convolving, 1)
                    for c in range(4):
                        for kt in range(KT):
                            for e in range(GE):
                                last = nc.tensor.matmul(conv[s % 2][64 * kt:64 * kt + 64, c],
                                                        band[:, s, kt, c, e], v_ch[:, s % 2, kt, c, :, 2 * e:2 * e + W],
                                                        start=e == 0, stop=e == GE - 1)
                    last.then_inc(convolved, 1)

        @block.vector
        def _(dve):
            with dve.Fori(0, GROUPS8 // 2) as j:
                for s in range(2):
                    dve.wait_ge(convolved, 2 * j + s + 1 + BANDS)
                    nc.vector.tensor_copy(gz[:, bass.ds(8 * j + 4 * s, 4)], conv[s][:]).then_inc(gz_copied, 1)


def turn_part(nc, gz, o_att, flip, osum, mlp_loads, mlp_weights_landed):
    with ExitStack() as ctx:
        flip_sb = ctx.enter_context(nc.sbuf_tensor("flip_sb", [P, P], F32))
        turned = [ctx.enter_context(nc.psum_tensor(f"turned{k}", [P, 4, KT, H], F32)) for k in range(4)]
        flip_landed = ctx.enter_context(nc.semaphore("flip_landed"))
        o_landed = [ctx.enter_context(nc.semaphore(f"o_landed{b}")) for b in range(B)]
        turned_done = ctx.enter_context(nc.semaphore("turned_done"))
        added = ctx.enter_context(nc.semaphore("added"))
        N = B * W // 4

        block = ctx.enter_context(nc.Block())

        @block.sync
        def _(sp):
            sp.dma_start(flip_sb[:], flip).then_inc(flip_landed, 16)
            for b in range(B):
                for kt in range(KT):
                    sp.dma_start(osum[:, kt, b * PIX:(b + 1) * PIX].rearrange("p (i n) -> p i n", i=CHUNKS),
                                 o_att[b, :, kt * P:(kt + 1) * P].rearrange("i p n -> p i n")).then_inc(o_landed[b], 16)
            for dst, src in mlp_loads:
                sp.dma_start(dst, src).then_inc(mlp_weights_landed, 16)

        @block.tensor
        def _(pe):
            pe.wait_ge(flip_landed, 16)
            for n in range(N):
                if n >= 4:
                    pe.wait_ge(added, n - 3)
                for j in range(4):
                    last = nc.tensor.matmul(turned[n % 4][:, j].rearrange("p k h -> p (k h)"), gz[:, :, 4 * n + j],
                                            flip_sb[:], start=True, stop=True)
                last.then_inc(turned_done, 1)

        @block.vector
        def _(dve):
            for n in range(N):
                b, w = divmod(4 * n, W)
                if w == 0:
                    dve.wait_ge(o_landed[b], 16 * KT)
                dve.wait_ge(turned_done, n + 1)
                for kt in range(KT):
                    o = osum[:, kt, b * PIX:(b + 1) * PIX].rearrange("p (i r w) -> p w r i", i=WS, r=WS)[:, w:w + 4]
                    last = nc.vector.tensor_tensor(o, turned[n % 4][:, :, kt].rearrange("p w (r i) -> p w r i", i=WS),
                                                   o, ALU.add)
                last.then_inc(added, 1)


def mlp_part(nc, x1, osum, projw_sb, fc1w_sb, fc2w_sb, vec_sb, weights_landed, out):
    with ExitStack() as ctx:
        def sb(name, shape, dt=F32):
            return ctx.enter_context(nc.sbuf_tensor("mlp_" + name, shape, dt))

        def sem(name):
            return ctx.enter_context(nc.semaphore("mlp_" + name))

        mean_w = sb("mean_w", [P, P])
        eps = sb("eps", [P, 1])
        x_in = sb("x_in", [P, 2, KT, CHUNK])
        xc = sb("xc", [P, KT, CHUNK])
        sq = sb("sq", [P, KT, CHUNK])
        std = sb("std", [P, CHUNK])
        rstd = sb("rstd", [P, CHUNK])
        xh = sb("xh", [P, KT, CHUNK])
        xn = sb("xn", [P, 2, KT, CHUNK])
        x2 = sb("x2", [P, 2, KT, CHUNK])
        hid = sb("hid", [P, FT, CHUNK])
        y = sb("y2", [P, KT, CHUNK])

        def bank(name):
            return ctx.enter_context(nc.psum_tensor("mlp_" + name, [P, 512], F32))

        pj = [bank("pj0"), bank("pj1")]
        sc = [bank("sc0"), bank("sc1")]
        tp = [bank("tp0"), bank("tp1")]
        ob = [bank("ob0"), bank("ob1")]

        setup_done = sem("setup_done")
        x_landed = [sem("xin_landed0"), sem("xin_landed1")]
        mean_done = sem("mean_done")
        centered = sem("centered")
        squared = sem("squared")
        var_done = sem("var_done")
        std_done = sem("std_done")
        rstd_done = sem("rstd_done")
        scaled = sem("scaled")
        xn_ready = sem("xn_ready")
        out_projected = sem("out_projected2")
        x2_ready = sem("x2_ready")
        fc1_done = sem("fc1_done")
        hid_ready = sem("hid_ready")
        fc2_done = sem("fc2_done")
        y_ready = sem("y_ready2")
        y_stored = sem("y_stored2")

        LOADS = 4

        def v(name, kt=0):
            return vec_sb[:, VEC[name] + kt:VEC[name] + kt + 1]

        def o_rows(kt, n):
            return osum[:, kt].rearrange("p (i r s c) -> p i r c s", i=B * CHUNKS, r=WS, s=WS)[
                :, bass.ds(n, 1)].squeeze(1)

        block = ctx.enter_context(nc.Block())


        @block.sync
        def _(sp):
            def load(b, i, k):
                sp.dma_start(x_in[:, k], x1[b].rearrange("(k p) n -> p k n", p=P)[
                    :, :, bass.ts(i, CHUNK)]).then_inc(x_landed[k], 16)

            def pair(b, i, following):
                for k in range(2):
                    n = b * CHUNKS + 2 * i + k
                    if following:
                        nb, ni = following
                        sp.wait_ge(x2_ready, n + 2)
                        load(nb, 2 * ni + k, k)
                    sp.wait_ge(y_ready, n + 2)
                    sp.dma_start(out[b].rearrange("(k p) n -> p k n", p=P)[:, :, bass.ts(2 * i + k, CHUNK)],
                                 y[:]).then_inc(y_stored, 16)
            load(0, 0, 0)
            load(0, 1, 1)
            for b in range(B):
                with sp.Fori(0, CHUNKS // 2 - 1) as i:
                    pair(b, i, (b, i + 1))
                pair(b, CHUNKS // 2 - 1, (b + 1, 0) if b + 1 < B else None)
            sp.wait_ge(y_stored, 16 * (B * CHUNKS + 1))

        @block.gpsimd
        def _(pool):
            for s in (centered, scaled, xn_ready, x2_ready, y_ready, fc2_done):
                pool.sem_inc(s, 1)
            pool.sem_inc(y_stored, 16)

        @block.tensor
        def _(pe):
            def project(n):
                for ct in range(KT):
                    for kt in range(KT):
                        last = nc.tensor.matmul(pj[ct][:], projw_sb[:, kt, ct * P:(ct + 1) * P],
                                                o_rows(kt, n), start=kt == 0, stop=kt == KT - 1)
                last.then_inc(out_projected, 1)

            def mean(n, k):
                pe.wait_ge(x2_ready, n + 2)
                for kt in range(KT):
                    last = nc.tensor.matmul(pj[0][:], mean_w[:], x2[:, k, kt], start=kt == 0, stop=kt == KT - 1)
                last.then_inc(mean_done, 1)

            def variance(n):
                pe.wait_ge(squared, n + 1)
                for kt in range(KT):
                    last = nc.tensor.matmul(pj[1][:], mean_w[:], sq[:, kt], start=kt == 0, stop=kt == KT - 1)
                last.then_inc(var_done, 1)

            banks = sc + tp

            def chunk(n, k, following):
                def fc1(ft):
                    if ft >= 4:
                        pe.wait_ge(hid_ready, n * FT + ft - 1)
                    for kt in range(KT):
                        last = nc.tensor.matmul(banks[ft % 4][:], fc1w_sb[:, kt, ft * P:(ft + 1) * P],
                                                xn[:, k, kt], start=kt == 0, stop=kt == KT - 1)
                    last.then_inc(fc1_done, 1)

                def fc2(ft):
                    if ft == 0:
                        pe.wait_ge(y_ready, n + 1)
                    pe.wait_ge(hid_ready, n * FT + ft + 3)
                    for ct in range(KT):
                        last = nc.tensor.matmul(ob[ct][:], fc2w_sb[:, ft, ct * P:(ct + 1) * P], hid[:, ft],
                                                start=ft == 0, stop=ft == FT - 1)
                    if ft == FT - 1:
                        last.then_inc(fc2_done, 1)
                pe.wait_ge(xn_ready, n + 2)
                for ft in range(FT):
                    fc1(ft)
                    if following:
                        if ft == 1:
                            project(n + 1)
                        if ft == 3:
                            mean(n + 1, 1 - k)
                        if ft == 5:
                            variance(n + 1)
                    if ft >= 2:
                        fc2(ft - 2)
                fc2(FT - 2)
                fc2(FT - 1)

            pe.wait_ge(weights_landed, 16 * LOADS)
            pe.wait_ge(setup_done, 1)
            project(0)
            mean(0, 0)
            variance(0)
            with pe.Fori(0, B * CHUNKS // 2 - 1) as j:
                for k in range(2):
                    chunk(2 * j + k, k, True)
            chunk(B * CHUNKS - 2, 0, True)
            chunk(B * CHUNKS - 1, 1, False)

        @block.scalar
        def _(act):
            act.sem_inc(hid_ready, 2)
            act.wait_ge(weights_landed, 16 * LOADS)
            act.wait_ge(setup_done, 1)

            def square(n):
                act.wait_ge(centered, n + 2)
                nc.scalar.activation(sq[:], xc[:], ACT.Square).then_inc(squared, 1)

            def deviation(n):
                act.wait_ge(var_done, n + 1)
                nc.scalar.activation(std[:], pj[1][:], ACT.Sqrt, bias=eps[:]).then_inc(std_done, 1)

            def affine(n, k):
                act.wait_ge(scaled, n + 2)
                for kt in range(KT):
                    last = nc.scalar.activation(xn[:, k, kt], xh[:, kt], ACT.Identity, scale=v("norm2_g", kt),
                                                bias=v("norm2_b", kt))
                last.then_inc(xn_ready, 1)

            def chunk(n, k, following):
                for ft in range(FT):
                    act.wait_ge(fc1_done, n * FT + ft + 1)
                    if ft == 0:
                        act.wait_ge(fc2_done, n + 1)
                    nc.scalar.activation(hid[:, ft], (sc + tp)[ft % 4][:], ACT.Gelu,
                                         bias=v("fc1_b", ft)).then_inc(hid_ready, 1)
                    if following:
                        if ft == 2:
                            square(n + 1)
                        if ft == 5:
                            deviation(n + 1)
                        if ft == 6:
                            affine(n + 1, 1 - k)

            square(0)
            deviation(0)
            affine(0, 0)
            with act.Fori(0, B * CHUNKS // 2 - 1) as j:
                for k in range(2):
                    chunk(2 * j + k, k, True)
            chunk(B * CHUNKS - 2, 0, True)
            chunk(B * CHUNKS - 1, 1, False)

        @block.vector
        def _(dve):
            nc.vector.memset(mean_w[:], 1.0 / C)
            nc.vector.memset(eps[:], EPS).then_inc(setup_done, 1)
            dve.wait_ge(weights_landed, 16 * LOADS)

            def norm(n, j, k):
                dve.wait_ge(out_projected, n + 1)
                dve.wait_ge(x_landed[k], 16 * (j + 1))
                for ct in range(KT):
                    last = nc.vector.scalar_tensor_tensor(x2[:, k, ct], pj[ct][:], v("proj_b", ct), x_in[:, k, ct],
                                                          ALU.add, ALU.add)
                last.then_inc(x2_ready, 1)
                dve.wait_ge(mean_done, n + 1)
                dve.wait_ge(scaled, n + 1)
                for kt in range(KT):
                    last = nc.vector.tensor_tensor(xc[:, kt], x2[:, k, kt], pj[0][:], ALU.subtract)
                last.then_inc(centered, 1)
                dve.wait_ge(std_done, n + 1)
                nc.vector.reciprocal(rstd[:], std[:]).then_inc(rstd_done, 1)
                dve.wait_ge(rstd_done, n + 1)
                dve.wait_ge(xn_ready, n + 1)
                for kt in range(KT):
                    last = nc.vector.tensor_tensor(xh[:, kt], xc[:, kt], rstd[:], ALU.mult)
                last.then_inc(scaled, 1)

            def chunk(n, k, following):
                if following is not None:
                    dve.wait_ge(y_ready, n + 1)
                    norm(n + 1, following, 1 - k)
                dve.wait_ge(fc2_done, n + 2)
                dve.wait_ge(y_stored, 16 * n + 16)
                for ct in range(KT):
                    last = nc.vector.scalar_tensor_tensor(y[:, ct], ob[ct][:], v("fc2_b", ct), x2[:, k, ct],
                                                          ALU.add, ALU.add)
                last.then_inc(y_ready, 1)

            norm(0, 0, 0)
            with dve.Fori(0, B * CHUNKS // 2 - 1) as j:
                chunk(2 * j, 0, j)
                chunk(2 * j + 1, 1, j + 1)
            chunk(B * CHUNKS - 2, 0, B * CHUNKS // 2 - 1)
            chunk(B * CHUNKS - 1, 1, None)


def program(nc, x, wqk, bqk, wg, wout, vec, ident, qkvw, bv, rpb, projw, taps, flip, fc1w, fc2w, out):
    x1 = nc.dram_tensor("x1_scratch", (B, C, PIX), F32).ap()
    nonlocal_part(nc, x, wqk, bqk, wg, wout, vec, ident, x1)
    v_img = nc.dram_tensor("v_scratch", (B, 4, H, W, 2 * QC), F32).ap()
    o_att = nc.dram_tensor("o_scratch", (B, CHUNKS, C, CHUNK), F32).ap()
    with ExitStack() as ctx:
        gz = ctx.enter_context(nc.sbuf_tensor("gz", [P, P, B * W], F32))
        band_landed = [ctx.enter_context(nc.semaphore(f"band_landed{k}")) for k in range(BANDS)]
        with nc.sbuf_tensor("band", [P, BANDS, KT, 4, GE, H], F32) as band:
            window_part(nc, x1, qkvw, bv, rpb, vec, ident, v_img, o_att, taps, band, band_landed)
            conv_part(nc, v_img, taps, band, band_landed, gz)
        osum = ctx.enter_context(nc.sbuf_tensor("osum", [P, KT, B * PIX], F32))
        projw_sb = ctx.enter_context(nc.sbuf_tensor("projw_sb", [P, KT, C], F32))
        fc1w_sb = ctx.enter_context(nc.sbuf_tensor("fc1w_sb", [P, KT, HID], F32))
        fc2w_sb = ctx.enter_context(nc.sbuf_tensor("fc2w_sb", [P, FT, C], F32))
        vec_sb = ctx.enter_context(nc.sbuf_tensor("vec_sb3", [P, NVEC], F32))
        mlp_weights_landed = ctx.enter_context(nc.semaphore("mlp_weights_landed"))
        turn_part(nc, gz, o_att, flip, osum, (
            (vec_sb[:], vec), (projw_sb[:], projw.rearrange("(k p) o -> p k o", p=P)),
            (fc1w_sb[:], fc1w.rearrange("(k p) o -> p k o", p=P)),
            (fc2w_sb[:], fc2w.rearrange("(k p) o -> p k o", p=P))), mlp_weights_landed)
        mlp_part(nc, x1, osum, projw_sb, fc1w_sb, fc2w_sb, vec_sb, mlp_weights_landed, out)


def kernel(**inputs):
    import numpy as np
    import concourse.bacc as bacc
    from concourse.bass_utils import run_bass_kernel_spmd

    a = {k: np.asarray(v) for k, v in inputs.items()}
    L0, L1 = "L0_conv_", "L1_conv_"

    def cols(v):
        return v.reshape(-1, P).T

    vec = np.concatenate([cols(v) for v in (
        a[L0 + "b_g"], a[L0 + "b_out"], a[L1 + "norm1_g"], a[L1 + "norm1_b"], a[L1 + "qkv_b"], a[L1 + "proj_b"],
        a[L1 + "gaze_b"], a[L1 + "norm2_g"], a[L1 + "norm2_b"], a[L1 + "fc1_b"], a[L1 + "fc2_b"])], axis=1)
    at = np.stack(np.meshgrid(np.arange(WS), np.arange(WS), indexing="ij")).reshape(2, -1)
    off = at[:, :, None] - at[:, None, :] + WS - 1
    rpb = a[L1 + "rpb_table"][off[0] * (2 * WS - 1) + off[1]]
    rpb = rpb.reshape(WS * WS, WS * WS, HP, 2).transpose(3, 0, 2, 1).reshape(P, HP * WS * WS)
    v_order = np.arange(C).reshape(2, 4, HD).transpose(1, 0, 2).ravel()
    taps = np.zeros((C, 2 * GE, LINE), np.float32)
    taps[:, :GK, H - GK // 2 - 1:H + GK // 2] = a[L1 + "gaze_w"][:, :, 0].transpose(2, 1, 0)
    flip = np.kron(np.eye(KT, dtype=np.float32), np.eye(H, dtype=np.float32)[::-1])
    arrays = {
        "x": a["x"].reshape(B, C, PIX),
        "wqk": np.concatenate([a[L0 + "w_theta"], a[L0 + "w_phi"]]).T,
        "bqk": np.broadcast_to(np.concatenate([a[L0 + "b_theta"], a[L0 + "b_phi"]]), (P, 2 * CH)),
        "wg": a[L0 + "w_g"].T,
        "wout": a[L0 + "w_out"].T,
        "vec": vec,
        "ident": np.eye(P, dtype=np.float32),
        "qkvw": np.concatenate([a[L1 + "qkv_w"][:2 * C], a[L1 + "qkv_w"][2 * C:][v_order]]).T,
        "bv": np.broadcast_to(a[L1 + "qkv_b"][2 * C:][v_order], (P, C)),
        "rpb": rpb,
        "projw": a[L1 + "proj_w"].T,
        "taps": taps,
        "flip": flip,
        "fc1w": a[L1 + "fc1_w"].T,
        "fc2w": a[L1 + "fc2_w"].T,
    }
    nc = bacc.Bacc("TRN2", target_bir_lowering=False, num_devices=1)
    fed, args = {}, []
    for name, v in arrays.items():
        v = np.ascontiguousarray(v)
        fed[f"in_{name}"] = v
        args.append(nc.dram_tensor(f"in_{name}", v.shape, mybir.dt.from_np(v.dtype), kind="ExternalInput").ap())
    args.append(nc.dram_tensor("out_x", (B, C, PIX), F32, kind="ExternalOutput").ap())
    program(nc, *args)
    r = run_bass_kernel_spmd(nc, [fed], core_ids=[0])
    return r.results[0]["out_x"].reshape(B, C, H, W)
```
